# Optimizing a Trainium2 kernel written in Bass

```python
import numpy as np
import jax
import jax.numpy as jnp

def _softmax(x, axis=-1):
    return jax.nn.softmax(x, axis=axis)

def _gelu(x):
    return jax.nn.gelu(x, approximate=True)

def _silu(x):
    return jax.nn.silu(x)

def _sigmoid(x):
    return jax.nn.sigmoid(x)

def _layernorm(x, axis=-1, eps=1e-05):
    m = jnp.mean(x, axis=axis, keepdims=True)
    v = jnp.var(x, axis=axis, keepdims=True)
    return (x - m) / jnp.sqrt(v + eps)

def _scatter_add(tgt, idx, src, axis=0):
    return tgt.at[idx].add(src)

def _segment_sum(src, seg, n):
    return jax.ops.segment_sum(src, seg, n)
kernel_name = 'mk_gnn_ffn_d1_gnn_r8_1ee2d4'

def setup_inputs(seed: int=0):
    np.random.seed(seed)
    _w = jnp.asarray

    def _rec_inputs():
        import jax
        import jax.numpy as jnp
        _gk = jax.random.key(seed)
        x = -0.0002117 + 1 * jax.random.normal(jax.random.fold_in(_gk, 1), (1250, 512), jnp.float32)
        _s = jax.random.randint(jax.random.fold_in(_gk, 2), (20000,), 0, 1250, jnp.int32)
        _d = jax.random.randint(jax.random.fold_in(_gk, 3), (20000,), 0, 1250, jnp.int32)
        _loop = jnp.arange(1250, dtype=jnp.int32)
        src = jnp.concatenate([_s, _d, _loop])
        dst = jnp.concatenate([_d, _s, _loop])
        _o = jnp.argsort(dst, stable=True)
        src = src[_o]
        dst = dst[_o]
        return (x, src, dst)
    x, src, dst = _rec_inputs()

    def _L0_gnn_setup():
        import jax, jax.numpy as jnp
        import numpy as np
        N = 6250
        IN_CH = 512
        OUT_CH = 512
        DEG = 32
        E = N * DEG
        key = jax.random.key(seed)
        kx, kwc, kwn, kb, ke = jax.random.split(key, 5)
        x = jax.random.normal(kx, (N, IN_CH), dtype=jnp.float32)
        bound = 1.0 / np.sqrt(IN_CH)
        wc = jax.random.uniform(kwc, (IN_CH, OUT_CH), minval=-bound, maxval=bound, dtype=jnp.float32)
        wn = jax.random.uniform(kwn, (IN_CH, OUT_CH), minval=-bound, maxval=bound, dtype=jnp.float32)
        bias = jax.random.uniform(kb, (OUT_CH,), minval=-bound, maxval=bound, dtype=jnp.float32)
        src = jnp.repeat(jnp.arange(N, dtype=jnp.int64), DEG)
        dst = jax.random.randint(ke, (E,), 0, N, dtype=jnp.int64)
        edge_index = jnp.stack([src, dst], axis=0)
        return {'x': x, 'wc': wc, 'wn': wn, 'bias': bias, 'edge_index': edge_index}
    _L0_gnn_all = _L0_gnn_setup()
    _L0_gnn_in = {k: v for k, v in _L0_gnn_all.items() if k in ('wc', 'wn', 'bias')}
    del _L0_gnn_all

    def _L0_ffn_setup():
        import jax, jax.numpy as jnp
        import numpy as np
        B, S, H, E, F = (4, 256, 512, 8, 512)
        key = jax.random.key(seed)
        k = jax.random.split(key, 7)
        x = jax.random.normal(k[0], (B, S, H), dtype=jnp.float32)
        Wr = jax.random.normal(k[1], (H, E), dtype=jnp.float32) / np.sqrt(H)
        br = jnp.zeros((E,), dtype=jnp.float32)
        W1 = jax.random.normal(k[2], (E, H, F), dtype=jnp.float32) / np.sqrt(H)
        b1 = jnp.zeros((E, F), dtype=jnp.float32)
        W2 = jax.random.normal(k[3], (E, F, H), dtype=jnp.float32) / np.sqrt(F)
        b2 = jnp.zeros((E, H), dtype=jnp.float32)
        return {'x': x, 'Wr': Wr, 'br': br, 'W1': W1, 'b1': b1, 'W2': W2, 'b2': b2}
    _L0_ffn_all = _L0_ffn_setup()
    _L0_ffn_in = {k: v for k, v in _L0_ffn_all.items() if k in ('Wr', 'br', 'W1', 'b1', 'W2', 'b2')}
    del _L0_ffn_all
    return {'x': x, 'src': src, 'dst': dst, 'L0_gnn_wc': _L0_gnn_in['wc'], 'L0_gnn_wn': _L0_gnn_in['wn'], 'L0_gnn_bias': _L0_gnn_in['bias'], 'L0_ffn_Wr': _L0_ffn_in['Wr'], 'L0_ffn_br': _L0_ffn_in['br'], 'L0_ffn_W1': _L0_ffn_in['W1'], 'L0_ffn_b1': _L0_ffn_in['b1'], 'L0_ffn_W2': _L0_ffn_in['W2'], 'L0_ffn_b2': _L0_ffn_in['b2']}

def reference(x, src, dst, L0_gnn_wc, L0_gnn_wn, L0_gnn_bias, L0_ffn_Wr, L0_ffn_br, L0_ffn_W1, L0_ffn_b1, L0_ffn_W2, L0_ffn_b2):
    import jax
    import jax.numpy as jnp

    def _L0_gnn_ref(x, wc, wn, bias, edge_index):
        import jax, jax.numpy as jnp
        import numpy as np
        N = 6250
        IN_CH = 512
        OUT_CH = 512
        DEG = 32
        E = N * DEG
        alpha = x @ wc
        beta = x @ wn
        src, dst = (edge_index[0], edge_index[1])
        sums = jax.ops.segment_sum(beta[dst], src, num_segments=x.shape[0])
        counts = jax.ops.segment_sum(jnp.ones_like(src, dtype=beta.dtype), src, num_segments=x.shape[0])
        gamma = sums / counts[:, None]
        return alpha + gamma + bias

    def _L0_ffn_ref(x, Wr, br, W1, b1, W2, b2):
        import jax, jax.numpy as jnp
        import numpy as np
        B, S, H, E, F = (4, 256, 512, 8, 512)
        b, s, h = x.shape
        xt = x.reshape(-1, h)
        logits = xt @ Wr + br
        probs = jax.nn.softmax(logits, axis=-1)
        G = jnp.max(probs, axis=-1)
        idx = jnp.argmax(probs, axis=-1)
        h1 = jax.nn.relu(jnp.einsum('nh,ehf->nef', xt, W1) + b1)
        eo = jnp.einsum('nef,efh->neh', h1, W2) + b2
        Eout = jnp.take_along_axis(eo, idx[:, None, None], axis=1)[:, 0, :]
        y = G[:, None] * Eout
        return y.reshape(b, s, h)
    edge_index = jnp.stack([src, dst])
    x = x + _L0_gnn_ref(_layernorm(x, axis=-1), L0_gnn_wc, L0_gnn_wn, L0_gnn_bias, edge_index)
    x = x + _L0_ffn_ref(_layernorm(x, axis=-1)[None], L0_ffn_Wr, L0_ffn_br, L0_ffn_W1, L0_ffn_b1, L0_ffn_W2, L0_ffn_b2)[0]
    return x

_drawn_inputs = setup_inputs


def setup_inputs(seed=0):
    import zlib

    import numpy as np

    out = dict(_drawn_inputs(seed))
    spreads = {'L0_ffn_br': (0.0, 0.1), 'L0_ffn_b1': (0.0, 0.348), 'L0_ffn_b2': (0.0, 0.1)}
    factors = {}
    for name, (base, spread) in spreads.items():
        noise = np.random.default_rng([zlib.crc32(name.encode()), seed]).standard_normal(out[name].shape)
        drawn = base * np.exp(spread * noise) if base else spread * noise
        out[name] = jnp.asarray(drawn.astype(out[name].dtype))
    for name, factor in factors.items():
        out[name] = (out[name] * factor).astype(out[name].dtype)
    return out
```

```python
import numpy as np
import concourse.bass as bass
from concourse import mybir
from contextlib import ExitStack

P = 128
H = 512
KC = H // P
N = 1250
E_EDGES = 41250
NEXP = 8
NT = -(-N // P)
LAST = N - (NT - 1) * P
NS = NT * P
ET = -(-E_EDGES // P)
TPC = 33
ETP = NT * TPC
GRP = 3
NG = TPC // GRP
SB = NT
MARGIN = 12
WIN = 28
WC = WIN * SB
QN = 32
QB = P // QN
QC = QN * SB
ROW = H + 4
TOKT = (N - NEXP) // P + NEXP
SLOTS = TOKT * P
PAD_SRC, PAD_DST = 16384, 8192
N_PAD_EDGES = ETP * P - E_EDGES
EPS = 1e-5
HB = NT // 2

BASE = [P * r // TPC - MARGIN for r in range(TPC)]


def segments(r):
    out, d = [], BASE[r]
    while d < BASE[r] + WIN:
        c, q = d // P, d % P // QN
        end = min(BASE[r] + WIN, (d // QN + 1) * QN)
        out.append((c, q, (d - BASE[r]) * SB, (end - d) * SB, d % QN * SB))
        d = end
    return out


OPEN = {}
CLOSE = {}
for _r in range(TPC):
    for _c, _q, _, _, _ in segments(_r):
        OPEN.setdefault((_c, _q), _r)
        CLOSE[(_c, _q)] = _r

T_ID = 0
T_TRI = T_ID + P
T_IOTA = T_TRI + P
T_BASE = T_IOTA + WC
T_VALID = T_BASE + ETP
T_PAD = T_VALID + NT
T_TOK = T_PAD + NT
T_KMOD = T_TOK + NT
T_FREE = T_KMOD + 1
T_COLS = T_FREE + 1
T_WIDE = HB * P


def tables():
    t = np.zeros((P, T_COLS + T_WIDE), np.float32)
    p = np.arange(P)
    t[:, T_ID:T_ID + P] = np.eye(P)
    t[:, T_TRI:T_TRI + P] = p[:, None] < p[None, :]
    t[:, T_IOTA:T_IOTA + WC] = np.arange(WC)
    t[:, T_BASE:T_BASE + ETP] = [SB * (P * i + b) for i in range(NT) for b in BASE]
    tok = P * np.arange(NT)[None, :] + p[:, None]
    t[:, T_VALID:T_VALID + NT] = tok < N
    t[:, T_PAD:T_PAD + NT] = tok >= N
    t[:, T_TOK:T_TOK + NT] = tok
    t[:, T_KMOD] = np.where(p < 3 * NEXP, p % NEXP, -1)
    t[:, T_FREE] = 1 << 20
    t[:, T_COLS:] = np.arange(T_WIDE)
    return t


def wait_for(eng, sem, n):
    if not isinstance(n, int) or n > 0:
        eng.wait_ge(sem, n)


class Chain:

    def __init__(self, eng, sem, base=0):
        self.eng, self.sem, self.base, self.n = eng, sem, base, 0

    def link(self, ins):
        self.n += 1
        ins.then_inc(self.sem, 1)
        self.eng.wait_ge(self.sem, self.base + self.n)


def build(nc, x, src, dst, wc, wn, bias, Wr, br, W1, b1, W2, b2, tab, out):
    f32, bf16, f16, i32 = mybir.dt.float32, mybir.dt.bfloat16, mybir.dt.float16, mybir.dt.int32
    ALU, ACT, AX = mybir.AluOpType, mybir.ActivationFunctionType, mybir.AxisListType.X

    beta_rows = nc.dram_tensor("beta_rows", (NS, H), f32, kind="Internal").ap()
    slot_rows = nc.dram_tensor("slot_rows", (SLOTS, ROW), f32, kind="Internal").ap()

    ctx = ExitStack()
    with ctx:
        def sb(name, shape, dt):
            return ctx.enter_context(nc.sbuf_tensor(name, shape, dt))

        def pb(name, shape, dt=f32):
            return ctx.enter_context(nc.psum_tensor(name, shape, dt))

        def sem(name):
            return ctx.enter_context(nc.semaphore(name))

        w1_sb = sb("w1_sb", [P, NEXP * KC * H], f32)
        w2_sb = sb("w2_sb", [P, NEXP * KC * H], f32)
        BP = 3 * NT * H
        beta = w2_sb[:, 0:BP // 2].bitcast(bf16).rearrange("p (a i n) -> p a i n", a=3, i=NT)
        OH = P + WC
        ring = w2_sb[:, BP // 2:BP // 2 + TPC * OH // 2].bitcast(bf16).rearrange("p (r c) -> p r c", r=TPC)
        mid = sb("mid", [P, NT * NS // 2 + 2 * KC * H], f32)
        adj = mid[:, 0:NT * NS // 2].bitcast(bf16).rearrange("p (i s) -> p i s", i=NT)
        wn_sb = mid[:, NT * NS // 2:NT * NS // 2 + KC * H].rearrange("p (k n) -> p k n", k=KC)
        wc_sb = mid[:, NT * NS // 2 + KC * H:].rearrange("p (k n) -> p k n", k=KC)
        rows = mid[:, 0:TOKT * ROW].rearrange("p (j c) -> p j c", j=TOKT)
        rows_i = mid[:, 0:TOKT * ROW].bitcast(i32).rearrange("p (j c) -> p j c", j=TOKT)
        wide_iota = mid[:, 0:T_WIDE]
        wide_hot = mid[:, T_WIDE:2 * T_WIDE]
        got_row = mid[:, 2 * T_WIDE:2 * T_WIDE + H]
        whole_beta = mid[:, 2 * T_WIDE + H:2 * T_WIDE + 2 * H]
        g0 = 2 * T_WIDE + 2 * H
        src_rel = mid[:, g0:g0 + ETP]
        gather_at = mid[:, g0 + ETP:g0 + 2 * ETP].bitcast(i32)
        xrow = sb("xrow", [P, NT * ROW], f32)
        X = xrow[:, :].rearrange("p (i c) -> p i c", i=NT)
        XI = xrow[:, :].bitcast(i32).rearrange("p (i c) -> p i c", i=NT)
        xT = sb("xT", [P, KC * P], f32)
        hid = xrow[:, 0:H]
        hidT = xrow[:, H:2 * H]
        y_out = xrow[:, 2 * H:3 * H]
        xn = sb("xn", [P, H], f32)
        bias_b = sb("bias_b", [P, H], f32)
        part = sb("part", [P, H], f32)
        chunk = sb("chunk", [P, SB, P], bf16)
        tabs = sb("tabs", [P, T_COLS], f32)
        ident = tabs[:, T_ID:T_ID + P]
        iota8 = tabs[:, T_IOTA:T_IOTA + NEXP]
        iota8_up = tabs[:, T_IOTA + NEXP:T_IOTA + 2 * NEXP]
        valid = tabs[:, T_VALID:T_VALID + NT]
        padding = tabs[:, T_PAD:T_PAD + NT]
        identb = sb("identb", [P, P], bf16)
        trib = sb("trib", [P, P], bf16)
        onesb = sb("onesb", [P, P], bf16)
        onesf = sb("onesf", [P, P], f32)
        iota16 = sb("iota16", [P, WC], f16)
        raw = w1_sb[:, 0:2 * 3 * P].bitcast(i32).rearrange("p (a c) -> p a c", a=2)
        rawf = w1_sb[:, 6 * P:12 * P].rearrange("p (a c) -> p a c", a=2)
        lane = w1_sb[:, 12 * P:12 * P + ETP].bitcast(i32)
        block_i = w1_sb[:, 16 * P:16 * P + ETP].bitcast(i32)
        missed = w1_sb[:, 20 * P:20 * P + ETP]
        e0 = BP // 2 + TPC * OH // 2
        src_i = w2_sb[:, e0:e0 + ETP].bitcast(i32)
        dst_f, lane_f, key = (w2_sb[:, e0 + k * ETP:e0 + (k + 1) * ETP] for k in (1, 2, 3))
        b2_sb = w2_sb[0:NEXP, e0 + 4 * ETP:e0 + 4 * ETP + H]
        assert e0 + 4 * ETP + H <= NEXP * KC * H
        stats = sb("stats", [P, NT, 6], f32)
        mv = sb("mv", [P, NT, 2], f32)
        std = sb("std", [P, NT], f32)
        rstd = sb("rstd", [P, NT], f32)
        taker = sb("taker", [P, 2], f32)
        eps = sb("eps", [P, 1], f32)
        zero_col = sb("zero_col", [P, 1], f32)
        bank_sums = sb("bank_sums", [P, NT * QB], f32)
        checks = sb("checks", [P, 2], f32)
        flag_f = sb("flag_f", [P, 1], f32)
        flag_i = sb("flag_i", [P, 1], i32)
        count = sb("count", [P, 1], f32)
        rcount = sb("rcount", [P, 1], f32)
        stat2 = sb("stat2", [P, 6], f32)
        mv2 = sb("mv2", [P, 2], f32)
        std2 = sb("std2", [P, 1], f32)
        gather_col = sb("gather_col", [P, 1], i32)
        wr_sb = sb("wr_sb", [P, KC, NEXP], f32)
        br_b = sb("br_b", [P, NEXP], f32)
        free_row = mid[:, NT * NS // 2 - ROW:NT * NS // 2]
        b1_rows = sb("b1_rows", [NEXP * KC, P], f32)
        b1T = sb("b1T", [P, NEXP * KC], f32)
        b2_rest = part[0:NEXP, :]
        b2_part = sb("b2_part", [NEXP, 3, H], bf16)
        b2_stack = sb("b2_stack", [P, H], bf16)
        def route(name, k=NEXP, dt=f32):
            return sb(name, [P, NT, k], dt)
        logit, eqmax, shifted, expo = route("logit"), route("eqmax"), route("shifted"), route("expo")
        hot, place = route("hot", dt=bf16), route("place")
        top, best, esum, slot_f = (sb(n, [P, NT], f32) for n in ("top", "best", "esum", "slot_f"))
        slot_i = sb("slot_i", [P, NT], i32)
        n_exp = sb("n_exp", [P, NEXP], i32)
        t_exp = sb("t_exp", [P, NEXP], i32)
        tiles_f = sb("tiles_f", [P, NEXP], f32)
        scan = [sb(f"scan{s}", [P, NEXP], f32) for s in range(3)]
        first_slot = sb("first_slot", [P, NEXP], f32)
        past = sb("past", [P, TOKT, NEXP], f32)
        exp_f = sb("exp_f", [P, TOKT], f32)
        exp_i = sb("exp_i", [P, TOKT], i32)
        exp_hot = sb("exp_hot", [P, TOKT, NEXP], f32)
        b1_sel = sb("b1_sel", [P, TOKT, KC], f32)
        b1_col = sb("b1_col", [P, KC], f32)
        pick = xrow[:, 4 * H:4 * H + TOKT * P // 2].bitcast(bf16).rearrange("p (j m) -> p j m", j=TOKT)
        row_at = sb("row_at", [P, 1], i32)

        bankA = [pb(f"bankA{q}", [P, H]) for q in range(QB)]
        bankT = pb("bankT", [P, H])
        bankB = pb("bankB", [P, H])
        bankC = pb("bankC", [P, H])
        bankR = pb("bankR", [P, 2 * H], bf16)
        bankRf = bankR[:, :].bitcast(f32)

        names = """edges_loaded tables_loaded small_loaded wn_loaded wc_loaded w1_loaded w2_loaded
            pad_rows_zero edge_pads_set iota_ready consts_ready edges_float edges_turned edges_turned_out
            var_ready std_ready rstd_ready xn_ready bias_added xT_turned xT_ready beta_done beta_hi beta_rest
            beta_mid beta_kept alpha_done alpha_added hot_ready tiles_done bank_out turned turned_out
            sums_checked checks_summed flag_ready dve_pre dve_in act_pre
            took took_slow sums_done x1_ready x1_kept dve_fast dve_slow var2_ready std2_ready xn2_ready xn2_turned xT2_ready logits_done
            shift_ready exp_ready chosen ranked dve_route slots_ready experts_ready b1_ready pick_ready
            b1_turned b2_parts b2_stacked free_ready slots_filled dispatched rows_loaded0 rows_loaded1
            xs_ready xs_turned xs_out h_done h_out h_turned hT_ready y_done y_ready row_ready y_stored
            beta_whole beta_stored wide_loaded slow_lists col_ready got_rows wide_ready edge_summed slow_x1
            act_relu pool_pre b1col_ready dve_ffn""".split()
        S = {n: sem(n) for n in names}
        x_loaded = [sem(f"x_loaded{i}") for i in range(NT)]

        def s(name):
            return S[name]

        w1v = w1_sb[:, :].rearrange("p (e k n) -> p e k n", e=NEXP, k=KC)
        w2v = w2_sb[:, :].rearrange("p (e k n) -> p e k n", e=NEXP, k=KC)

        block = ctx.enter_context(nc.Block())

        @block.sync
        def _(sp):
            sp.wait_ge(s("edge_pads_set"), 1)
            for a, ids in enumerate((src, dst)):
                for c in range(2):
                    sp.dma_start(raw[:, a, c * P:(c + 1) * P],
                                 ids[c * P * P:(c + 1) * P * P].rearrange("(t e) -> t e", e=P)).then_inc(s("edges_loaded"), 16)
                full = (E_EDGES - 2 * P * P) // P
                at = (2 * P + full) * P
                sp.dma_start(raw[0:full, a, 2 * P:3 * P],
                             ids[2 * P * P:at].rearrange("(t e) -> t e", e=P)).then_inc(s("edges_loaded"), 16)
                sp.dma_start(raw[full:full + 1, a, 2 * P:2 * P + E_EDGES - at],
                             ids[at:E_EDGES].rearrange("(t e) -> t e", t=1)).then_inc(s("edges_loaded"), 16)
            for i in range(NT):
                n = P if i < NT - 1 else LAST
                if i == NT - 1:
                    sp.wait_ge(s("pad_rows_zero"), 1)
                sp.dma_start(X[0:n, i, 0:H], x[i * P:i * P + n, :]).then_inc(x_loaded[i], 16)
                if i == 0:
                    sp.dma_start(wn_sb, wn.rearrange("(k p) n -> p k n", p=P)).then_inc(s("wn_loaded"), 16)
                    sp.dma_start(wc_sb, wc.rearrange("(k p) n -> p k n", p=P)).then_inc(s("wc_loaded"), 16)
            sp.wait_ge(s("free_ready"), 2)
            for j in range(TOKT):
                sp.dma_start(slot_rows[j * P:(j + 1) * P, :], free_row).then_inc(s("slots_filled"), 16)
            sp.wait_ge(s("iota_ready"), 2)
            for e in range(NEXP):
                sp.dma_start(w1v[:, e], W1[e].rearrange("(k p) n -> p k n", p=P)).then_inc(s("w1_loaded"), 16)
            sp.wait_ge(s("flag_ready"), 1)
            slow = sp.value_load(flag_i[0:1, 0:1], min_val=0, max_val=1 << 30)
            with sp.If(slow == 0):
                sp.wait_ge(s("sums_done"), NT)
            with sp.Else():
                sp.dma_start(wide_iota, tab[:, T_COLS:]).then_inc(s("wide_loaded"), 16)

                def store_beta(i):
                    sp.wait_ge(s("beta_whole"), i + 1)
                    sp.dma_start(beta_rows[bass.ds(i * P, P), :], whole_beta).then_inc(s("beta_stored"), 16)
                with sp.Fori(0, NT) as i:
                    store_beta(i)
                sp.wait_ge(s("slow_x1"), NT)
            sp.wait_ge(s("b2_parts"), 3)
            for e in range(NEXP):
                sp.dma_start(w2v[:, e], W2[e].rearrange("(k p) n -> p k n", p=P)).then_inc(s("w2_loaded"), 16)
            sp.wait_ge(s("dispatched"), 16 * NT)
            rv = slot_rows.rearrange("(j p) c -> p j c", p=P)
            sp.dma_start(rows[:, 0:1, :], rv[:, 0:1, :]).then_inc(s("rows_loaded0"), 16)
            sp.dma_start(rows[:, 1:TOKT, :], rv[:, 1:TOKT, :]).then_inc(s("rows_loaded1"), 16)
            sp.wait_ge(s("y_stored"), 16 * TOKT)

        @block.gpsimd
        def _(pool):
            pool.memset(raw[:, 0, 2 * P:3 * P], PAD_SRC)
            pool.memset(raw[:, 1, 2 * P:3 * P], PAD_DST).then_inc(s("edge_pads_set"), 1)
            pool.memset(onesb[:, :], 1.0)
            pool.memset(onesf[:, :], 1.0)
            pool.memset(eps[:, :], EPS)
            pool.memset(zero_col[:, :], 0.0)
            pool.memset(b2_stack[:, :], 0.0).then_inc(s("consts_ready"), 1)
            pool.memset(free_row, 0.0).then_inc(s("free_ready"), 1)
            pool.dma_start(tabs[:, :], tab[:, 0:T_COLS]).then_inc(s("tables_loaded"), 16)
            pool.dma_start(bias_b[:, :], bias.partition_broadcast(P)).then_inc(s("small_loaded"), 16)
            pool.dma_start(br_b[:, :], br.partition_broadcast(P)).then_inc(s("small_loaded"), 16)
            pool.dma_start(wr_sb[:, :, :], Wr.rearrange("(k p) n -> p k n", p=P)).then_inc(s("small_loaded"), 16)
            pool.dma_start(b1_rows[:, :], b1.rearrange("e (c p) -> (e c) p", p=P)).then_inc(s("small_loaded"), 16)
            pool.dma_start(b2_sb, b2).then_inc(s("small_loaded"), 16)
            pool.wait_ge(s("tables_loaded"), 16)
            pool.wait_ge(s("free_ready"), 1)
            pool.tensor_copy(free_row[:, H + 3:H + 4].bitcast(i32), tabs[:, T_FREE:T_FREE + 1]).then_inc(s("free_ready"), 1)
            pool.tensor_copy(XI[:, :, H + 3:H + 4], tabs[:, T_TOK:T_TOK + NT].unsqueeze(2)).then_inc(s("pool_pre"), 1)

            def take_wait(took):
                pool.tensor_tensor(taker[:, 1:2], eps[:, :], eps[:, :], ALU.add).then_inc(took, 1)
            last_node, last_beta = pool.to_reg(N - 1), pool.to_reg(NS - 1)
            pool.wait_ge(s("small_loaded"), 80)
            with pool.Fori(0, NT) as i:
                pool.wait_ge(s("xn_ready"), i + 1)
                pool.tensor_tensor(X[:, bass.ds(i, 1), 0:H].squeeze(1), X[:, bass.ds(i, 1), 0:H].squeeze(1),
                                   bias_b[:, :], ALU.add).then_inc(s("bias_added"), 1)
            pool.wait_ge(s("b2_parts"), 3)
            pool.wait_ge(s("consts_ready"), 1)
            for a in range(3):
                pool.dma_start(b2_stack[a * NEXP:(a + 1) * NEXP, :], b2_part[:, a, :]).then_inc(s("b2_stacked"), 16)
            pool.wait_ge(s("flag_ready"), 1)
            slow = pool.value_load(flag_i[0:1, 0:1], min_val=0, max_val=1 << 30)
            with pool.If(slow == 0):
                pool.nop()
            with pool.Else():
                pool.wait_ge(s("beta_stored"), 16 * NT)
                pool.wait_ge(s("slow_lists"), 2)
                def gather(t, h):
                    wait_for(pool, s("edge_summed"), t + h * ETP)
                    pool.tensor_copy(gather_col[:, :], gather_at[:, bass.ds(t, 1)]).then_inc(s("col_ready"), 1)
                    wait_for(pool, s("took_slow"), t + h * ETP)
                    pool.wait_ge(s("col_ready"), t + (h * ETP + 1))
                    take_wait(s("took_slow"))
                    pool.indirect_dma_start(got_row, None, beta_rows,
                                            bass.IndirectOffsetOnAxis(ap=gather_col[:, :], axis=0),
                                            bounds_check=last_beta, oob_is_err=False).then_inc(s("got_rows"), 16)
                for h in range(2):
                    gather(0, h)
                    with pool.Fori(1, ETP) as t:
                        gather(t, h)
            pool.nop()
            pool.wait_ge(s("slots_ready"), 1)
            pool.wait_ge(s("slots_filled"), 16 * TOKT)
            for i in range(NT):
                pool.indirect_dma_start(slot_rows, bass.IndirectOffsetOnAxis(ap=slot_i[:, i:i + 1], axis=0),
                                        X[:, i, :], None, bounds_check=SLOTS - 1,
                                        oob_is_err=False).then_inc(s("dispatched"), 16)
            def store_result(j):
                wait_for(pool, s("took"), j)
                pool.wait_ge(s("y_ready"), j + 1)
                take_wait(s("took"))
                pool.indirect_dma_start(out, bass.IndirectOffsetOnAxis(ap=row_at[:, :], axis=0), y_out, None,
                                        bounds_check=last_node, oob_is_err=False).then_inc(s("y_stored"), 16)
            store_result(0)
            with pool.Fori(1, TOKT) as j:
                store_result(j)

        @block.scalar
        def _(act):
            def bank_evac(c, q):
                nc.scalar.activation(chunk[:, :, q * QN:(q + 1) * QN],
                                     bankA[q][:, 0:QC].rearrange("p (d s) -> p s d", s=SB), ACT.Copy,
                                     accum_out=bank_sums[:, bass.ds(c * QB + q, 1)]).then_inc(s("bank_out"), 1)

            def turned_evac(c, half):
                act.wait_ge(s("turned"), c * 2 + (half + 1))
                nc.scalar.activation(adj[:, bass.ds(c, 1), half * (NS // 2):(half + 1) * (NS // 2)].squeeze(1),
                                     bankR[:, 0:NS // 2], ACT.Copy).then_inc(s("turned_out"), 1)

            act.wait_ge(s("consts_ready"), 1)
            act.wait_ge(s("var_ready"), 1)
            nc.scalar.activation(std[:, :], mv[:, :, 1], ACT.Sqrt, bias=eps[:, 0:1]).then_inc(s("std_ready"), 1)

            def body(i, first):
                act.wait_ge(s("xT_turned"), i + 1)
                if not first:
                    act.wait_ge(s("alpha_done"), i)
                nc.scalar.copy(xT[:, :], bankT[:, :]).then_inc(s("xT_ready"), 1)
                if not first:
                    act.wait_ge(s("tiles_done"), i * NG + (CLOSE[(-1, QB - 1)] // GRP + 1))
                    bank_evac(i - 1, QB - 1)
                act.wait_ge(s("beta_done"), i + 1)
                nc.scalar.copy(beta[:, 0, bass.ds(i, 1), :].squeeze(1), bankB[:, :]).then_inc(s("beta_hi"), 1)
                if not first:
                    turned_evac(i - 1, 0)
                act.wait_ge(s("beta_rest"), i + 1)
                nc.scalar.copy(beta[:, 1, bass.ds(i, 1), :].squeeze(1), part[:, :]).then_inc(s("beta_mid"), 1)
                if not first:
                    turned_evac(i - 1, 1)
                for q in range(QB - 1):
                    act.wait_ge(s("tiles_done"), i * NG + (CLOSE[(0, q)] // GRP + 1))
                    bank_evac(i, q)

            body(0, True)
            with act.Fori(1, NT) as i:
                body(i, False)
            act.wait_ge(s("tiles_done"), NT * NG)
            bank_evac(NT - 1, QB - 1)
            act.wait_ge(s("slots_filled"), 16 * TOKT)
            turned_evac(NT - 1, 0)
            turned_evac(NT - 1, 1)

            def second_norm(i):
                act.wait_ge(s("var2_ready"), i + 1)
                nc.scalar.activation(std2[:, :], mv2[:, 1:2], ACT.Sqrt, bias=eps[:, 0:1]).then_inc(s("std2_ready"), 1)
                nc.scalar.copy(X[:, bass.ds(i, 1), 0:H].squeeze(1), part[:, :]).then_inc(s("x1_kept"), 1)
                act.wait_ge(s("xn2_turned"), i + 1)
                wait_for(act, s("logits_done"), i)
                nc.scalar.copy(xT[:, :], bankT[:, :]).then_inc(s("xT2_ready"), 1)

            act.wait_ge(s("flag_ready"), 1)
            slow = act.value_load(flag_i[0:1, 0:1], min_val=0, max_val=1 << 30)
            with act.If(slow == 0):
                second_norm(0)
                with act.Fori(1, NT) as i:
                    second_norm(i)
            with act.Else():
                second_norm(0)
                with act.Fori(1, NT) as i:
                    second_norm(i)
            act.nop()

            act.wait_ge(s("shift_ready"), 1)
            nc.scalar.activation(expo[:, :, :], shifted[:, :, :], ACT.Exp).then_inc(s("exp_ready"), 1)

            def xs_evac(j):
                act.wait_ge(s("xs_turned"), j + 1)
                nc.scalar.copy(xT[:, :], bankT[:, :]).then_inc(s("xs_out"), 1)

            def relu(j):
                act.wait_ge(s("h_turned"), j + 1)
                act.wait_ge(s("b1col_ready"), j + 1)
                for c in range(KC):
                    last = nc.scalar.activation(hidT[:, c * P:(c + 1) * P], bankC[:, c * P:(c + 1) * P], ACT.Relu,
                                                bias=b1_col[:, c:c + 1])
                last.then_inc(s("hT_ready"), 1)

            xs_evac(0)
            with act.Fori(0, TOKT - 1) as j:
                xs_evac(j + 1)
                relu(j)
            relu(TOKT - 1)

        @block.vector
        def _(dve):
            V = nc.vector
            ch = Chain(dve, s("dve_pre"))
            V.memset(X[96:P, NT - 1, 0:H], 0.0).then_inc(s("pad_rows_zero"), 1)
            dve.wait_ge(s("tables_loaded"), 16)
            V.tensor_copy(iota16[:, :], tabs[:, T_IOTA:T_IOTA + WC])
            V.tensor_copy(identb[:, :], ident)
            V.tensor_copy(trib[:, :], tabs[:, T_TRI:T_TRI + P]).then_inc(s("iota_ready"), 1)
            dve.wait_ge(s("edges_loaded"), 16 * 8)
            V.tensor_copy(rawf, raw).then_inc(s("edges_float"), 1)
            for i in range(4):
                dve.wait_ge(x_loaded[i], 16)
                V.bn_stats(stats[:, i, :], X[:, i, 0:H])
            dve.wait_ge(s("edges_turned"), 1)
            ch.link(V.tensor_copy(src_i, bankA[0][:, 0:ETP]))
            V.tensor_copy(dst_f, bankA[1][:, 0:ETP]).then_inc(s("edges_turned_out"), 1)
            V.tensor_scalar(lane, src_i, P - 1, None, ALU.bitwise_and)
            ch.link(V.tensor_scalar(block_i, src_i, 7, None, ALU.arith_shift_right))
            V.tensor_copy(lane_f[:, :], lane)
            dve.wait_ge(s("edges_turned_out"), 1)
            ch.link(V.scalar_tensor_tensor(key, dst_f, float(SB), block_i, ALU.mult, ALU.add))
            ch.link(V.tensor_tensor(key, key, tabs[:, T_BASE:T_BASE + ETP], ALU.subtract))
            ch.link(V.tensor_scalar(missed, key, float(WC), None, ALU.is_ge))
            ch.link(V.scalar_tensor_tensor(missed, key, 0.0, missed, ALU.is_lt, ALU.add))
            V.tensor_reduce(checks[:, 0:1], missed, AX, ALU.add).then_inc(s("iota_ready"), 1)
            for i in range(4, NT):
                dve.wait_ge(x_loaded[i], 16)
                last = V.bn_stats(stats[:, i, :], X[:, i, 0:H])
            ch.link(last)
            for i in range(NT):
                last = V.bn_aggr(mv[:, i, :], stats[:, i, :])
            last.then_inc(s("var_ready"), 1)
            dve.wait_ge(s("std_ready"), 1)
            V.reciprocal(rstd[:, :], std[:, :]).then_inc(s("rstd_ready"), 1)
            dve.wait_ge(s("rstd_ready"), 1)

            def body(i, first):
                if not first:
                    dve.wait_ge(s("xT_turned"), i)
                V.tensor_scalar(xn[:, :], X[:, bass.ds(i, 1), 0:H].squeeze(1), mv[:, bass.ds(i, 1), 0],
                                rstd[:, bass.ds(i, 1)], ALU.subtract, ALU.mult).then_inc(s("xn_ready"), 1)
                for g in range(NG):
                    if not first:
                        dve.wait_ge(s("tiles_done"), i * NG + (g + 1 - NG))
                    for r in range(g * GRP, (g + 1) * GRP):
                        V.tensor_scalar(ring[:, r, 0:P], iota16[:, 0:P], lane_f[:, bass.ds(i * TPC + r, 1)], None,
                                        ALU.is_equal)
                        last = V.tensor_scalar(ring[:, r, P:OH], iota16[:, :], key[:, bass.ds(i * TPC + r, 1)], None,
                                               ALU.is_equal)
                    last.then_inc(s("hot_ready"), 1)
                    if g == 4:
                        dve.wait_ge(s("beta_hi"), i + 1)
                        V.tensor_tensor(part[:, :], bankB[:, :], beta[:, 0, bass.ds(i, 1), :].squeeze(1),
                                        ALU.subtract).then_inc(s("beta_rest"), 1)
                    if g == 7:
                        dve.wait_ge(s("beta_mid"), i + 1)
                        V.tensor_tensor(beta[:, 2, bass.ds(i, 1), :].squeeze(1), part[:, :],
                                        beta[:, 1, bass.ds(i, 1), :].squeeze(1), ALU.subtract).then_inc(s("beta_kept"), 1)
                        dve.wait_ge(s("alpha_done"), i + 1)
                        dve.wait_ge(s("bias_added"), i + 1)
                        V.tensor_tensor(X[:, bass.ds(i, 1), 0:H].squeeze(1), X[:, bass.ds(i, 1), 0:H].squeeze(1),
                                        bankC[:, :], ALU.add).then_inc(s("alpha_added"), 1)

            body(0, True)
            with dve.Fori(1, NT) as i:
                body(i, False)

            dve.wait_ge(s("small_loaded"), 80)
            V.tensor_copy(b2_part[:, 0, :], b2_sb).then_inc(s("b2_parts"), 1)
            dve.wait_ge(s("b2_parts"), 1)
            ch.link(V.tensor_tensor(b2_rest, b2_sb, b2_part[:, 0, :], ALU.subtract))
            V.tensor_copy(b2_part[:, 1, :], b2_rest).then_inc(s("b2_parts"), 1)
            dve.wait_ge(s("b2_parts"), 2)
            V.tensor_tensor(b2_part[:, 2, :], b2_rest, b2_part[:, 1, :], ALU.subtract).then_inc(s("b2_parts"), 1)

            dve.wait_ge(s("bank_out"), NT * QB)
            ch.link(V.tensor_reduce(count[:, :], bank_sums[:, :], AX, ALU.max))
            V.tensor_scalar(checks[:, 1:2], count[:, :], 256.0, None, ALU.is_ge).then_inc(s("sums_checked"), 1)
            dve.wait_ge(s("checks_summed"), 1)
            ch.link(V.tensor_reduce(flag_f[:, :], bankB[:, 0:2], AX, ALU.add))
            V.tensor_scalar(flag_i[:, :], flag_f[:, :], float(N_PAD_EDGES), None, ALU.subtract).then_inc(s("flag_ready"), 1)
            dve.wait_ge(s("b1_turned"), 1)
            V.tensor_copy(b1T[:, :], bankC[:, 0:NEXP * KC]).then_inc(s("b1_ready"), 1)

            def second_norm(i, ch):
                ch.link(V.bn_stats(stat2[:, :], part[:, :]))
                V.tensor_copy(taker[:, 0:1], stat2[:, 0:1])
                V.bn_aggr(mv2[:, 0:2], stat2[:, :]).then_inc(s("var2_ready"), 1)
                dve.wait_ge(s("std2_ready"), i + 1)
                ch.link(V.reciprocal(mv2[:, 1:2], std2[:, :]))
                wait_for(dve, s("xn2_turned"), i)
                V.tensor_scalar(xn[:, :], part[:, :], mv2[:, 0:1], mv2[:, 1:2], ALU.subtract, ALU.mult).then_inc(s("xn2_ready"), 1)
                V.tensor_copy(X[:, bass.ds(i, 1), H:H + 2].squeeze(1), mv2[:, :])

            dve.wait_ge(s("flag_ready"), 1)
            slow = dve.value_load(flag_i[0:1, 0:1], min_val=0, max_val=1 << 30)
            with dve.If(slow == 0):
                def graph_out(i, par):
                    c = Chain(dve, s("dve_fast"), i * 4)
                    Xi = X[:, bass.ds(i, 1), 0:H].squeeze(1)
                    dve.wait_ge(s("sums_done"), i + 1)
                    c.link(V.tensor_tensor(count[:, :], bankA[2 + par][:, 0:1], padding[:, bass.ds(i, 1)], ALU.add))
                    c.link(V.reciprocal(rcount[:, :], count[:, :]))
                    wait_for(dve, s("x1_kept"), i)
                    V.scalar_tensor_tensor(part[:, :], bankA[par][:, :], rcount[:, 0:1], Xi, ALU.mult, ALU.add).then_inc(s("x1_ready"), 1)
                    dve.wait_ge(s("x1_ready"), i + 1)
                    second_norm(i, c)
                    assert c.n == 4
                graph_out(0, 0)
                graph_out(1, 1)
                with dve.Fori(1, NT // 2) as m:
                    for par in range(2):
                        graph_out(m * 2 + par, par)
            with dve.Else():
                def rejoin(i):
                    c = Chain(dve, s("dve_slow"), i)
                    c.link(V.tensor_tensor(part[:, :], beta[:, 0, bass.ds(i, 1), :].squeeze(1),
                                           beta[:, 1, bass.ds(i, 1), :].squeeze(1), ALU.add))
                    wait_for(dve, s("beta_stored"), i * 16)
                    V.tensor_tensor(whole_beta, part[:, :], beta[:, 2, bass.ds(i, 1), :].squeeze(1),
                                    ALU.add).then_inc(s("beta_whole"), 1)
                rejoin(0)
                with dve.Fori(1, NT) as i:
                    rejoin(i)
                V.tensor_scalar(gather_at, dst_f, float(NS - 1), None, ALU.min).then_inc(s("slow_lists"), 1)
                dve.wait_ge(s("wide_loaded"), 16)
                for h in range(2):
                    V.tensor_scalar(src_rel, src_i, float(h * T_WIDE), None, ALU.subtract).then_inc(s("slow_lists"), 1)
                    dve.wait_ge(s("slow_lists"), 2 + h)
                    def wide(t):
                        wait_for(dve, s("edge_summed"), t + h * ETP)
                        V.tensor_scalar(wide_hot, wide_iota, src_rel[:, bass.ds(t, 1)], None,
                                        ALU.is_equal).then_inc(s("wide_ready"), 1)
                    wide(0)
                    with dve.Fori(1, ETP) as t:
                        wide(t)
                    dve.wait_ge(s("edge_summed"), (h + 1) * ETP)
                    c = Chain(dve, s("dve_slow"), NT + 2 * HB * h)
                    sums = [bankA[0], bankA[1], bankA[2], bankA[3], bankT]
                    for b in range(HB):
                        i = h * HB + b
                        c.link(V.tensor_tensor(count[:, :], bankB[:, b:b + 1], padding[:, i:i + 1], ALU.add))
                        c.link(V.reciprocal(rcount[:, :], count[:, :]))
                        V.scalar_tensor_tensor(X[:, i, 0:H], sums[b][:, :], rcount[:, 0:1], X[:, i, 0:H],
                                               ALU.mult, ALU.add).then_inc(s("slow_x1"), 1)
                dve.wait_ge(s("slow_x1"), NT)
                def block_norm(i):
                    wait_for(dve, s("x1_kept"), i)
                    V.tensor_copy(part[:, :], X[:, bass.ds(i, 1), 0:H].squeeze(1)).then_inc(s("x1_ready"), 1)
                    dve.wait_ge(s("x1_ready"), i + 1)
                    second_norm(i, Chain(dve, s("dve_slow"), NT + 4 * HB + i * 2))
                block_norm(0)
                with dve.Fori(1, NT) as i:
                    block_norm(i)
            dve.nop()

            ch = Chain(dve, s("dve_route"))
            dve.wait_ge(s("logits_done"), NT)
            full = [P, NT, NEXP]

            def over_exp(ap):
                return ap.unsqueeze(2).broadcast_to(full)

            def over_tiles(ap):
                return ap.unsqueeze(1).broadcast_to(full)
            logits = bankB[:, 0:NT * NEXP].rearrange("p (i e) -> p i e", e=NEXP)
            ch.link(V.tensor_tensor(logit[:, :, :], logits, over_tiles(br_b[:, :]), ALU.add))
            ch.link(V.tensor_reduce(top[:, :], logit[:, :, :], AX, ALU.max))
            V.tensor_tensor(shifted[:, :, :], logit[:, :, :], over_exp(top[:, :]), ALU.subtract).then_inc(s("shift_ready"), 1)
            ch.link(V.tensor_tensor(eqmax[:, :, :], logit[:, :, :], over_exp(top[:, :]), ALU.is_equal))
            ch.link(V.scalar_tensor_tensor(place[:, :, :], eqmax[:, :, :], -float(NEXP), over_tiles(iota8_up), ALU.mult, ALU.add))
            ch.link(V.tensor_reduce(best[:, :], place[:, :, :], AX, ALU.min))
            ch.link(V.tensor_scalar(best[:, :], best[:, :], float(NEXP - 1), None, ALU.min))
            ch.link(V.tensor_tensor(eqmax[:, :, :], over_tiles(iota8), over_exp(best[:, :]), ALU.is_equal))
            V.tensor_tensor(hot[:, :, :], eqmax[:, :, :], over_exp(valid), ALU.mult).then_inc(s("chosen"), 1)
            dve.wait_ge(s("exp_ready"), 1)
            ch.link(V.tensor_reduce(esum[:, :], expo[:, :, :], AX, ALU.add))
            dve.wait_ge(s("x1_kept"), NT)
            V.reciprocal(X[:, :, H + 2:H + 3].squeeze(2), esum[:, :])
            dve.wait_ge(s("ranked"), 1)
            ch.link(V.tensor_scalar(n_exp[:, :], bankC[:, P:P + NEXP], float(P - 1), None, ALU.add))
            ch.link(V.tensor_scalar(t_exp[:, :], n_exp[:, :], 7, None, ALU.arith_shift_right))
            ch.link(V.tensor_copy(tiles_f[:, :], t_exp[:, :]))
            prev = tiles_f
            for k, step in enumerate((1, 2, 4)):
                V.tensor_copy(scan[k][:, 0:step], prev[:, 0:step])
                ch.link(V.tensor_tensor(scan[k][:, step:], prev[:, step:], prev[:, 0:NEXP - step], ALU.add))
                prev = scan[k]
            tiles_to = scan[2]
            ch.link(V.tensor_tensor(first_slot[:, :], tiles_to[:, :], tiles_f[:, :], ALU.subtract))
            ch.link(V.scalar_tensor_tensor(place[:, :, :], over_tiles(first_slot[:, :]), float(P),
                                           bankC[:, 0:NT * NEXP].rearrange("p (i e) -> p i e", e=NEXP), ALU.mult, ALU.add))
            ch.link(V.tensor_tensor(place[:, :, :], place[:, :, :], hot[:, :, :], ALU.mult))
            ch.link(V.tensor_reduce(slot_f[:, :], place[:, :, :], AX, ALU.add))
            V.scalar_tensor_tensor(slot_i[:, :], padding, float(2 * SLOTS), slot_f[:, :], ALU.mult,
                                   ALU.add).then_inc(s("slots_ready"), 1)
            ft = [P, TOKT, NEXP]
            ch.link(V.tensor_tensor(past[:, :, :], tabs[:, T_IOTA:T_IOTA + TOKT].unsqueeze(2).broadcast_to(ft),
                                    tiles_to[:, :].unsqueeze(1).broadcast_to(ft), ALU.is_ge))
            ch.link(V.tensor_reduce(exp_f[:, :], past[:, :, :], AX, ALU.add))
            ch.link(V.tensor_scalar(exp_f[:, :], exp_f[:, :], float(NEXP - 1), None, ALU.min))
            V.tensor_copy(exp_i[:, :], exp_f[:, :]).then_inc(s("experts_ready"), 1)
            ch.link(V.tensor_tensor(exp_hot[:, :, :], iota8.unsqueeze(1).broadcast_to(ft),
                                    exp_f[:, :].unsqueeze(2).broadcast_to(ft), ALU.is_equal))
            dve.wait_ge(s("b1_ready"), 1)
            b1v = b1T[:, :].rearrange("p (e c) -> p c e", c=KC)
            assert TOKT * NEXP <= H
            for c in range(KC):
                prod = (bias_b, part)[c % 2][:, 0:TOKT * NEXP].rearrange("p (j e) -> p j e", e=NEXP)
                ch.link(V.tensor_tensor(prod, exp_hot[:, :, :], b1v[:, c:c + 1, :].broadcast_to(ft), ALU.mult))
                last = V.tensor_reduce(b1_sel[:, :, c:c + 1].squeeze(2), prod, AX, ALU.add)
            ch.link(last)

            def xs_norm(j):
                wait_for(dve, s("xs_turned"), j)
                r = rows[:, bass.ds(j, 1), :].squeeze(1)
                V.tensor_scalar(xn[:, :], r[:, 0:H], r[:, H:H + 1], r[:, H + 1:H + 2], ALU.subtract,
                                ALU.mult).then_inc(s("xs_ready"), 1)

            def h_evac(j):
                dve.wait_ge(s("h_done"), j + 1)
                V.tensor_copy(hid, bankB[:, :]).then_inc(s("h_out"), 1)
                wait_for(dve, s("hT_ready"), j)
                V.tensor_copy(b1_col[:, :], b1_sel[:, bass.ds(j, 1), :].squeeze(1)).then_inc(s("b1col_ready"), 1)

            def result(j):
                dve.wait_ge(s("y_done"), j + 1)
                wait_for(dve, s("y_stored"), j * 16)
                r = rows[:, bass.ds(j, 1), :].squeeze(1)
                V.tensor_copy(row_at[:, :], rows_i[:, bass.ds(j, 1), H + 3:H + 4].squeeze(1))
                V.scalar_tensor_tensor(y_out, bankA[0][:, :], r[:, H + 2:H + 3], r[:, 0:H], ALU.mult,
                                       ALU.add).then_inc(s("y_ready"), 1)

            dve.wait_ge(s("rows_loaded0"), 16)
            xs_norm(0)
            V.tensor_scalar(pick[:, :, :], exp_f[:, :].unsqueeze(2).broadcast_to([P, TOKT, P]),
                            tabs[:, T_KMOD:T_KMOD + 1], None, ALU.is_equal).then_inc(s("pick_ready"), 1)
            dve.wait_ge(s("rows_loaded1"), 16)
            xs_norm(1)
            h_evac(0)

            def step(j):
                xs_norm(j + 1)
                h_evac(j)
                result(j - 1)
            step(1)
            with dve.Fori(2, TOKT - 1) as j:
                step(j)
            h_evac(TOKT - 1)
            result(TOKT - 2)
            result(TOKT - 1)

        @block.tensor
        def _(pe):
            mm = nc.tensor.matmul
            pe.wait_ge(s("edges_float"), 1)
            pe.wait_ge(s("tables_loaded"), 16)
            for a in range(2):
                for c in range(3):
                    last = nc.tensor.transpose(bankA[a][:, c * P:(c + 1) * P], rawf[:, a, c * P:(c + 1) * P], ident)
            last.then_inc(s("edges_turned"), 1)

            def turn(c, half):
                pe.wait_ge(s("bank_out"), (c + 1) * QB)
                wait_for(pe, s("turned_out"), c * 2 + half)
                for b in range(HB):
                    last = nc.tensor.transpose(bankR[:, b * P:(b + 1) * P], chunk[:, half * HB + b, :], identb[:, :])
                last.then_inc(s("turned"), 1)

            def tiles(i, g, first, final):
                pe.wait_ge(s("hot_ready"), i * NG + (g + 1))
                for r in range(g * GRP, (g + 1) * GRP):
                    for c, q, k0, n, col in segments(r):
                        if (c < 0 and first) or (c > 0 and final):
                            continue
                        start = OPEN[(c, q)] == r and c >= 0 and not (c == 0 and (1, q) in OPEN and not first)
                        if start:
                            if c == 1:
                                pe.wait_ge(s("bank_out"), i * QB + (q + 1))
                            elif not first:
                                pe.wait_ge(s("bank_out"), i * QB + (q + 1 - QB))
                        last = mm(bankA[q][:, col:col + n], ring[:, r, 0:P], ring[:, r, P + k0:P + k0 + n],
                                  start=start, stop=True, skip_group_check=True)
                last.then_inc(s("tiles_done"), 1)

            def body(i, first=False, final=False):
                pe.wait_ge(s("xn_ready"), i + 1)
                for c in range(KC):
                    last = nc.tensor.transpose(bankT[:, c * P:(c + 1) * P], xn[:, c * P:(c + 1) * P], ident)
                last.then_inc(s("xT_turned"), 1)
                if first:
                    pe.wait_ge(s("iota_ready"), 1)
                    pe.wait_ge(s("edges_turned_out"), 1)
                tiles(i, 0, first, final)
                tiles(i, 1, first, final)
                pe.wait_ge(s("xT_ready"), i + 1)
                if first:
                    pe.wait_ge(s("wn_loaded"), 16)
                else:
                    pe.wait_ge(s("beta_rest"), i)
                for c in range(KC):
                    last = mm(bankB[:, :], xT[:, c * P:(c + 1) * P], wn_sb[:, c, :], start=c == 0, stop=c == KC - 1)
                last.then_inc(s("beta_done"), 1)
                tiles(i, 2, first, final)
                tiles(i, 3, first, final)
                if not first:
                    turn(i - 1, 0)
                if first:
                    pe.wait_ge(s("wc_loaded"), 16)
                else:
                    pe.wait_ge(s("alpha_added"), i)
                for c in range(KC):
                    last = mm(bankC[:, :], xT[:, c * P:(c + 1) * P], wc_sb[:, c, :], start=c == 0, stop=c == KC - 1)
                last.then_inc(s("alpha_done"), 1)
                tiles(i, 4, first, final)
                tiles(i, 5, first, final)
                if not first:
                    turn(i - 1, 1)
                for g in range(6, NG):
                    tiles(i, g, first, final)

            body(0, first=True)
            body(1)
            with pe.Fori(2, NT - 1) as i:
                body(i)
            body(NT - 1, final=True)
            pe.wait_ge(s("alpha_added"), NT)
            pe.wait_ge(s("small_loaded"), 80)
            nc.tensor.transpose(bankC[:, 0:NEXP * KC], b1_rows[:, :], ident[0:NEXP * KC, 0:NEXP * KC]).then_inc(s("b1_turned"), 1)
            turn(NT - 1, 0)
            pe.wait_ge(s("sums_checked"), 1)
            pe.wait_ge(s("beta_rest"), NT)
            mm(bankB[:, 0:2], onesf[:, :], checks[:, :], start=True, stop=True).then_inc(s("checks_summed"), 1)
            turn(NT - 1, 1)
            pe.wait_ge(s("turned_out"), 2 * NT)

            def second_turn(i):
                pe.wait_ge(s("xn2_ready"), i + 1)
                for c in range(KC):
                    last = nc.tensor.transpose(bankT[:, c * P:(c + 1) * P], xn[:, c * P:(c + 1) * P], ident)
                last.then_inc(s("xn2_turned"), 1)

            def router(i):
                pe.wait_ge(s("xT2_ready"), i + 1)
                for c in range(KC):
                    last = mm(bankB[:, bass.ds(i * NEXP, NEXP)], xT[:, c * P:(c + 1) * P], wr_sb[:, c, :],
                              start=c == 0, stop=c == KC - 1)
                last.then_inc(s("logits_done"), 1)

            pe.wait_ge(s("beta_kept"), NT)
            pe.wait_ge(s("flag_ready"), 1)
            slow = pe.value_load(flag_i[0:1, 0:1], min_val=0, max_val=1 << 30)
            with pe.If(slow == 0):
                def sums(i, par, first=False):
                    lhs = [adj[:, d, bass.ds(i * P, P)] for d in range(NT)]
                    for d in range(NT):
                        mm(bankA[2 + par][:, 0:1], lhs[d], onesb[:, 0:1], start=d == 0, stop=d == NT - 1,
                           skip_group_check=True)
                    for d in range(NT):
                        for a in range(3):
                            last = mm(bankA[par][:, :], lhs[d], beta[:, a, d, :], start=d == 0 and a == 0,
                                      stop=d == NT - 1 and a == 2)
                        if d == HB and not first:
                            second_turn(i - 1)
                    last.then_inc(s("sums_done"), 1)
                    if not first:
                        router(i - 1)
                sums(0, 0, first=True)
                sums(1, 1)
                with pe.Fori(1, NT // 2) as m:
                    for par in range(2):
                        pe.wait_ge(s("x1_ready"), m * 2 + (par - 1))
                        sums(m * 2 + par, par)
                second_turn(NT - 1)
                router(NT - 1)
            with pe.Else():
                acc = [bankA[0], bankA[1], bankA[2], bankA[3], bankT]

                def edge(t, first=False):
                    pe.wait_ge(s("got_rows"), (t + 1) * 16)
                    pe.wait_ge(s("wide_ready"), t + 1)
                    for b in range(HB):
                        hot_b = wide_hot[:, b * P:(b + 1) * P]
                        mm(acc[b][:, :], hot_b, got_row, start=first, stop=True, skip_group_check=True)
                        last = mm(bankB[:, b:b + 1], hot_b, onesf[:, 0:1], start=first and b == 0, stop=True,
                                  skip_group_check=True)
                    last.then_inc(s("edge_summed"), 1)
                for h in range(2):
                    if h:
                        pe.wait_ge(s("slow_x1"), HB)
                    edge(h * ETP, first=True)
                    with pe.Fori(1, ETP) as t:
                        edge(t + h * ETP)
                pe.wait_ge(s("slow_x1"), NT)
                with pe.Fori(0, NT) as i:
                    second_turn(i)
                    router(i)
            pe.nop()

            pe.wait_ge(s("chosen"), 1)
            hv = hot[:, :, :].rearrange("p i e -> p (i e)")
            W = NT * NEXP
            mm(bankC[:, 0:W], trib[:, :], hv, start=True, stop=True, skip_group_check=True)
            for k in range(1, NT):
                mm(bankC[:, k * NEXP:W], onesb[:, :], hv[:, 0:W - k * NEXP], start=False, stop=True,
                   skip_group_check=True)
            for k in range(NT):
                last = mm(bankC[:, P:P + NEXP], onesb[:, :], hv[:, k * NEXP:(k + 1) * NEXP], start=False, stop=True,
                          skip_group_check=True)
            last.then_inc(s("ranked"), 1)

            def xs_turn(j):
                pe.wait_ge(s("xs_ready"), j + 1)
                for c in range(KC):
                    last = nc.tensor.transpose(bankT[:, c * P:(c + 1) * P], xn[:, c * P:(c + 1) * P], ident)
                last.then_inc(s("xs_turned"), 1)

            def expert_of(j):
                return pe.value_load(exp_i[0:1, bass.ds(j, 1)], min_val=0, max_val=NEXP - 1)

            def up(j):
                e = expert_of(j)
                pe.wait_ge(s("xs_out"), j + 1)
                for c in range(KC):
                    last = mm(bankB[:, :], xT[:, c * P:(c + 1) * P], w1_sb[:, bass.ds(e * (KC * H) + c * H, H)],
                              start=c == 0, stop=c == KC - 1)
                last.then_inc(s("h_done"), 1)

            def down(j):
                e = expert_of(j)
                pe.wait_ge(s("hT_ready"), j + 1)
                wait_for(pe, s("y_ready"), j)
                mm(bankA[0][:, :], pick[:, bass.ds(j, 1), :].squeeze(1), b2_stack[:, :], start=True, stop=False)
                for c in range(KC):
                    last = mm(bankA[0][:, :], hidT[:, c * P:(c + 1) * P], w2_sb[:, bass.ds(e * (KC * H) + c * H, H)],
                              start=False, stop=c == KC - 1)
                last.then_inc(s("y_done"), 1)

            def h_turn(j):
                pe.wait_ge(s("h_out"), j + 1)
                for c in range(KC):
                    last = nc.tensor.transpose(bankC[:, c * P:(c + 1) * P], hid[:, c * P:(c + 1) * P], ident)
                last.then_inc(s("h_turned"), 1)

            pe.wait_ge(s("experts_ready"), 1)
            xs_turn(0)
            pe.wait_ge(s("w1_loaded"), 16 * NEXP)
            up(0)
            xs_turn(1)
            h_turn(0)
            pe.wait_ge(s("pick_ready"), 1)
            pe.wait_ge(s("b2_stacked"), 48)
            up(1)
            xs_turn(2)
            pe.wait_ge(s("w2_loaded"), 16 * NEXP)
            down(0)
            h_turn(1)
            with pe.Fori(2, TOKT - 1) as j:
                up(j)
                xs_turn(j + 1)
                down(j - 1)
                h_turn(j)
            up(TOKT - 1)
            down(TOKT - 2)
            h_turn(TOKT - 1)
            down(TOKT - 1)


_INS = ['x', 'src', 'dst', 'L0_gnn_wc', 'L0_gnn_wn', 'L0_gnn_bias', 'L0_ffn_Wr', 'L0_ffn_br', 'L0_ffn_W1', 'L0_ffn_b1',
        'L0_ffn_W2', 'L0_ffn_b2']


def kernel(**inputs):
    import concourse.bacc as _bacc
    from concourse.bass_utils import run_bass_kernel_spmd as _run

    nc = _bacc.Bacc("TRN2", target_bir_lowering=False, num_devices=1, dynamic_dma_scratch_size=8192)
    arrays, args = {}, []
    for name in _INS:
        a = np.ascontiguousarray(inputs[name])
        arrays[f"in_{name}"] = a
        args.append(nc.dram_tensor(f"in_{name}", a.shape, mybir.dt.from_np(a.dtype), kind="ExternalInput").ap())
    t = tables()
    arrays["tables"] = t
    args.append(nc.dram_tensor("tables", t.shape, mybir.dt.float32, kind="ExternalInput").ap())
    args.append(nc.dram_tensor("result", (N, H), mybir.dt.float32, kind="ExternalOutput").ap())
    build(nc, *args)
    r = _run(nc, [arrays], core_ids=[0])
    return r.results[0]["result"]
```

```python
import numpy as np
import concourse.bass as bass
from concourse import mybir
from contextlib import ExitStack

P = 128
H = 512
KC = H // P
N = 1250
E_EDGES = 41250
NEXP = 8
NT = -(-N // P)
LAST = N - (NT - 1) * P
NS = NT * P
ET = -(-E_EDGES // P)
TPC = 33
ETP = NT * TPC
GRP = 3
NG = TPC // GRP
SB = NT
MARGIN = 12
WIN = 28
WC = WIN * SB
QN = 32
QB = P // QN
QC = QN * SB
ROW = H + 2
TOKT = (N - NEXP) // P + NEXP
SLOTS = TOKT * P
PAD_SRC, PAD_DST = 16384, 8192
N_PAD_EDGES = ETP * P - E_EDGES
EPS = 1e-5
HB = NT // 2
TURN = 4
ROUNDS = -(-SB // TURN)
NPAY = 6
AHEAD = 4
ADJ_EXACT = 2048
ACT_TILES = [r for r in range(TPC) if (r + 1) * 16 // TPC > r * 16 // TPC]

BASE = [P * r // TPC - MARGIN for r in range(TPC)]


def segments(r):
    out, d = [], BASE[r]
    while d < BASE[r] + WIN:
        c, q = d // P, d % P // QN
        end = min(BASE[r] + WIN, (d // QN + 1) * QN)
        out.append((c, q, (d - BASE[r]) * SB, (end - d) * SB, d % QN * SB))
        d = end
    return out


OPEN = {}
CLOSE = {}
for _r in range(TPC):
    for _c, _q, _, _, _ in segments(_r):
        OPEN.setdefault((_c, _q), _r)
        CLOSE[(_c, _q)] = _r

T_ID = 0
T_TRI = T_ID + P
T_IOTA = T_TRI + P
T_BASE = T_IOTA + WC
T_PAD = T_BASE + ETP
T_PAY = T_PAD + NT
T_PLACE = T_PAY + NT * NPAY
T_KMOD = T_PLACE + NT * NEXP
T_DIFF = T_KMOD + 1
T_TRI8 = T_DIFF + P
T_COLS = T_TRI8 + NEXP * NEXP
T_WIDE = HB * P


def tables():
    t = np.zeros((P, T_COLS + T_WIDE), np.float32)
    p = np.arange(P)
    t[:, T_ID:T_ID + P] = np.eye(P)
    t[:, T_TRI:T_TRI + P] = p[:, None] < p[None, :]
    t[:, T_IOTA:T_IOTA + WC] = np.arange(WC)
    t[:, T_BASE:T_BASE + ETP] = [SB * (P * i + b) for i in range(NT) for b in BASE]
    tok = P * np.arange(NT)[None, :] + p[:, None]
    t[:, T_PAD:T_PAD + NT] = tok >= N
    pay = np.zeros((P, NT, NPAY))
    pay[:, :, 0], pay[:, :, 1], pay[:, :, 2] = np.arange(NT)[None, :], p[:, None], 1
    t[:, T_PAY:T_PAY + NT * NPAY] = pay.reshape(P, -1)
    t[:, T_PLACE:T_KMOD] = (np.arange(NEXP) + NEXP - 1 + 8 * NEXP * (tok >= N)[:, :, None]).reshape(P, -1)
    t[:, T_KMOD] = np.where(p < 3 * NEXP, p % NEXP, -1)
    d = np.eye(P) / 2 - np.eye(P, k=-1) / 2
    d[0, P - 1] = 0.5
    t[:, T_DIFF:T_DIFF + P] = d
    t[:, T_TRI8:T_COLS] = np.tril(np.ones((NEXP, NEXP)), -1).reshape(-1)
    t[:, T_COLS:] = np.arange(T_WIDE)
    return t


def wait_for(eng, sem, n):
    if not isinstance(n, int) or n > 0:
        eng.wait_ge(sem, n)


class Chain:

    def __init__(self, eng, sem, base=0):
        self.eng, self.sem, self.base, self.n = eng, sem, base, 0

    def link(self, ins):
        self.n += 1
        ins.then_inc(self.sem, 1)
        self.eng.wait_ge(self.sem, self.base + self.n)


def build(nc, x, src, dst, wc, wn, bias, Wr, br, W1, b1, W2, b2, tab, out):
    f32, bf16, f16, i32 = mybir.dt.float32, mybir.dt.bfloat16, mybir.dt.float16, mybir.dt.int32
    f32r = mybir.dt.float32r
    ALU, ACT, AX = mybir.AluOpType, mybir.ActivationFunctionType, mybir.AxisListType.X

    beta_rows = nc.dram_tensor("beta_rows", (NS, H), f32, kind="Internal").ap()
    node_rows = nc.dram_tensor("node_rows", (NS, ROW), f32, kind="Internal").ap()

    ctx = ExitStack()
    with ctx:
        def sb(name, shape, dt):
            return ctx.enter_context(nc.sbuf_tensor(name, shape, dt))

        def pb(name, shape, dt=f32):
            return ctx.enter_context(nc.psum_tensor(name, shape, dt))

        def sem(name):
            return ctx.enter_context(nc.semaphore(name))

        OH = P + WC
        with nc.sbuf_tensor("beta", [P, 2, NT, H], f32r) as beta:
            with nc.sbuf_tensor("ring", [P, TPC, OH], bf16) as ring:
                with nc.sbuf_tensor("lists", [P, 4 * ETP + H], f32) as lists:
                    pass
        W1_LATE = -(-(2 * NT * H + 4 * ETP + H + TPC * OH // 2 - NEXP * KC * H) // (KC * H))
        W2_LATE = -(-2 * NT * H // (KC * H))
        w2_sb = sb("w2_sb", [P, NEXP * KC * H], f32)
        w1_sb = sb("w1_sb", [P, NEXP * KC * H], f32)
        with nc.sbuf_tensor("adj", [P, NT, NS], f16) as adj:
            with nc.sbuf_tensor("w_graph", [P, 2, KC, H], f32) as w_graph:
                pass
            with nc.sbuf_tensor("lhs", [P, 2, NT, P], f32r) as lhs:
                pass
        wn_sb, wc_sb = w_graph[:, 0, :, :], w_graph[:, 1, :, :]
        mid = sb("mid", [P, NT * NS // 2 + 2 * KC * H], f32)
        rows = mid[:, 0:TOKT * ROW].rearrange("p (j c) -> p j c", j=TOKT)
        wide_iota = mid[:, 0:T_WIDE]
        wide_hot = mid[:, T_WIDE:2 * T_WIDE]
        got_row = mid[:, 2 * T_WIDE:2 * T_WIDE + H]
        whole_beta = mid[:, 2 * T_WIDE + H:2 * T_WIDE + 2 * H]
        g0 = 2 * T_WIDE + 2 * H
        src_rel = mid[:, g0:g0 + ETP]
        gather_at = mid[:, g0 + ETP:g0 + 2 * ETP].bitcast(i32)
        xrow = sb("xrow", [P, NT * ROW], f32)
        X = xrow[:, :].rearrange("p (i c) -> p i c", i=NT)
        xT = sb("xT", [P, KC * P], f32)
        hid = xrow[:, 0:H]
        hidT = xrow[:, H:2 * H]
        y_out = xrow[:, 2 * H:3 * H]
        xn = sb("xn", [P, H], f32)
        bias_b = sb("bias_b", [P, H], f32)
        part = sb("part", [P, H], f32)
        chunk = sb("chunk", [P, SB, P], f16)
        lane_hot = chunk[:, :, :].bitcast(bf16)
        tabs = sb("tabs", [P, T_COLS], f32)
        ident = tabs[:, T_ID:T_ID + P]
        iota8 = tabs[:, T_IOTA:T_IOTA + NEXP]
        not_top = tabs[:, T_PLACE:T_PLACE + NT * NEXP].rearrange("p (i e) -> p i e", i=NT)
        tri8 = tabs[:, T_TRI8:T_COLS].rearrange("p (e f) -> p e f", e=NEXP)
        padding = tabs[:, T_PAD:T_PAD + NT]
        diff = sb("diff", [P, P], f16)
        trib = sb("trib", [P, P], bf16)
        onesb = sb("onesb", [P, P], bf16)
        onesf = sb("onesf", [P, P], f32)
        iota16 = sb("iota16", [P, WC], f16)
        r0 = W1_LATE * KC * H
        raw = w1_sb[:, r0:r0 + 2 * 3 * P].bitcast(i32).rearrange("p (a c) -> p a c", a=2)
        rawf = w1_sb[:, r0 + 6 * P:r0 + 12 * P].rearrange("p (a c) -> p a c", a=2)
        lane = w1_sb[:, r0 + 12 * P:r0 + 12 * P + ETP].bitcast(i32)
        block_i = w1_sb[:, r0 + 16 * P:r0 + 16 * P + ETP].bitcast(i32)
        missed = w1_sb[:, r0 + 20 * P:r0 + 20 * P + ETP]
        src_i = lists[:, 0:ETP].bitcast(i32)
        dst_f, lane_f, key = (lists[:, k * ETP:(k + 1) * ETP] for k in (1, 2, 3))
        b2_sb = lists[0:NEXP, 4 * ETP:4 * ETP + H]
        lane_half = sb("lane_half", [P, ETP], f32)
        stats = sb("stats", [P, 6], f32)
        mv = sb("mv", [P, 2], f32)
        std = sb("std", [P, 1], f32)
        rstd = sb("rstd", [P, 1], f32)
        taker = sb("taker", [P, 3], f32)
        eps = sb("eps", [P, 1], f32)
        zero_col = sb("zero_col", [P, 1], f32)
        bank_sums = sb("bank_sums", [P, NT * QB], f32)
        checks = sb("checks", [P, 2], f32)
        flag_f = sb("flag_f", [P, 1], f32)
        flag_i = sb("flag_i", [P, 1], i32)
        count = sb("count", [P, 1], f32)
        rcount = sb("rcount", [P, 1], f32)
        stat2 = sb("stat2", [P, 6], f32)
        mv2 = sb("mv2", [P, 2], f32)
        std2 = sb("std2", [P, 1], f32)
        gather_col = sb("gather_col", [P, 1], i32)
        wr_sb = sb("wr_sb", [P, KC, NEXP], f32)
        br_b = sb("br_b", [P, NEXP], f32)
        b1_rows = sb("b1_rows", [NEXP * KC, P], f32)
        b1T = sb("b1T", [P, NEXP * KC], f32)
        b2_rest = part[0:NEXP, :]
        b2_part = sb("b2_part", [NEXP, 3, H], bf16)
        b2_stack = sb("b2_stack", [P, H], bf16)
        used = [TOKT * ROW]

        def carve(n):
            used[0] += n
            assert used[0] <= NT * NS // 2 + 2 * KC * H
            return mid[:, used[0] - n:used[0]]
        logit, eqmax, shifted, expo, place = (carve(NT * NEXP).rearrange("p (i e) -> p i e", i=NT) for _ in range(5))
        hot = sb("hot", [P, NT, NEXP], bf16)
        top, best, esum, slot_f = (sb(n, [P, NT], f32) for n in ("top", "best", "esum", "slot_f"))
        slot_i = sb("slot_i", [P, NT], i32)
        n_exp = sb("n_exp", [P, NEXP], i32)
        t_exp = sb("t_exp", [P, NEXP], i32)
        tiles_f = sb("tiles_f", [P, NEXP], f32)
        before = sb("before", [P, NEXP, NEXP], f32)
        tiles_to = sb("tiles_to", [P, NEXP], f32)
        first_slot = sb("first_slot", [P, NEXP], f32)
        past = carve(TOKT * NEXP).rearrange("p (j e) -> p j e", j=TOKT)
        exp_f = sb("exp_f", [P, TOKT], f32)
        exp_i = sb("exp_i", [P, TOKT], i32)
        exp_hot = carve(TOKT * NEXP).rearrange("p (j e) -> p j e", j=TOKT)
        b1_sel = sb("b1_sel", [P, TOKT, KC], f32)
        b1_col = sb("b1_col", [P, KC], f32)
        pick = xrow[:, 4 * H:4 * H + TOKT * P // 2].bitcast(bf16).rearrange("p (j m) -> p j m", j=TOKT)
        row_at = sb("row_at", [P, 1], i32)
        gate = sb("gate", [P, NT], f32)
        gate_rest = sb("gate_rest", [P, NT], f32)
        pay = sb("pay", [P, NT, NPAY], bf16)
        slot_tile, slot_lane = sb("slot_tile", [P, NT], i32), sb("slot_lane", [P, NT], i32)
        slot_tile_f, slot_lane_f = sb("slot_tile_f", [P, NT], f32), sb("slot_lane_f", [P, NT], f32)
        tile_hot = carve(NT * TOKT).rearrange("p (i j) -> p i j", i=NT)
        sent = carve(NT * NPAY * TOKT // 2).bitcast(bf16).rearrange("p (i v j) -> p i v j", i=NT, v=NPAY)
        got = carve(NPAY * TOKT).rearrange("p (v j) -> p v j", v=NPAY)
        node_f, out_f = sb("node_f", [P, TOKT], f32), sb("out_f", [P, TOKT], f32)
        node_i, out_i = sb("node_i", [P, TOKT], i32), sb("out_i", [P, TOKT], i32)
        gate_s = sb("gate_s", [P, TOKT], f32)

        bankA = [pb(f"bankA{q}", [P, H]) for q in range(QB)]
        bankT = pb("bankT", [P, H])
        bankB = pb("bankB", [P, H])
        bankC = pb("bankC", [P, H])
        bankR = pb("bankR", [P, H])

        names = """edges_loaded tables_loaded small_loaded wn_loaded wc_loaded w1_loaded w2_loaded
            pad_rows_zero edge_pads_set iota_ready consts_ready edges_float edges_turned edges_turned_out
            stats_ready var_ready std_ready rstd_ready xn_ready bias_added xT_turned xT_ready beta_done beta_hi beta_rest
            lhs_ready alpha_done alpha_added hot_ready tiles_done bank_out turned turned_out
            sums_checked checks_summed flag_ready dve_pre dve_in act_pre
            took took_slow sums_done x1_ready x1_kept dve_fast dve_slow var2_ready std2_ready xn2_ready xn2_turned xT2_ready logits_done
            shift_ready exp_ready chosen ranked dve_route slots_ready experts_ready b1_ready pick_ready
            b1_turned b2_parts b2_stacked stairs_ready rows_kept rows_stored later_rows sent_ready at_slots nodes_ready diff_ready
            xs_ready xs_turned xs_out h_done h_out h_turned hT_ready y_done y_ready row_ready y_stored
            beta_whole beta_stored wide_loaded slow_lists col_ready got_rows wide_ready edge_summed slow_x1
            act_relu pool_pre b1col_ready dve_ffn""".split()
        S = {n: sem(n) for n in names}
        x_loaded = [sem(f"x_loaded{i}") for i in range(NT)]
        rows_got = [sem(f"rows_got{j}") for j in range(AHEAD)]

        def s(name):
            return S[name]

        w1v = w1_sb[:, :].rearrange("p (e k n) -> p e k n", e=NEXP, k=KC)
        w2v = w2_sb[:, :].rearrange("p (e k n) -> p e k n", e=NEXP, k=KC)

        block = ctx.enter_context(nc.Block())

        @block.sync
        def _(sp):
            sp.dma_start(X[:, 0, 0:H], x[0:P, :]).then_inc(x_loaded[0], 16)
            sp.wait_ge(s("edge_pads_set"), 1)
            for a, ids in enumerate((src, dst)):
                for c in range(2):
                    sp.dma_start(raw[:, a, c * P:(c + 1) * P],
                                 ids[c * P * P:(c + 1) * P * P].rearrange("(t e) -> t e", e=P)).then_inc(s("edges_loaded"), 16)
                full = (E_EDGES - 2 * P * P) // P
                at = (2 * P + full) * P
                sp.dma_start(raw[0:full, a, 2 * P:3 * P],
                             ids[2 * P * P:at].rearrange("(t e) -> t e", e=P)).then_inc(s("edges_loaded"), 16)
                sp.dma_start(raw[full:full + 1, a, 2 * P:2 * P + E_EDGES - at],
                             ids[at:E_EDGES].rearrange("(t e) -> t e", t=1)).then_inc(s("edges_loaded"), 16)
            sp.dma_start(wn_sb, wn.rearrange("(k p) n -> p k n", p=P)).then_inc(s("wn_loaded"), 16)
            sp.dma_start(wc_sb, wc.rearrange("(k p) n -> p k n", p=P)).then_inc(s("wc_loaded"), 16)
            for i in range(1, NT):
                n = P if i < NT - 1 else LAST
                if i == NT - 1:
                    sp.wait_ge(s("pad_rows_zero"), 1)
                sp.dma_start(X[0:n, i, 0:H], x[i * P:i * P + n, :]).then_inc(x_loaded[i], 16)
            sp.wait_ge(s("iota_ready"), 3)
            for e in range(W1_LATE, NEXP):
                sp.dma_start(w1v[:, e], W1[e].rearrange("(k p) n -> p k n", p=P)).then_inc(s("w1_loaded"), 16)
            sp.wait_ge(s("tiles_done"), NT * NG)
            sp.wait_ge(s("b2_parts"), 3)

            def after_ring():
                for e in range(W1_LATE):
                    sp.dma_start(w1v[:, e], W1[e].rearrange("(k p) n -> p k n", p=P)).then_inc(s("w1_loaded"), 16)
                for e in range(W2_LATE, NEXP):
                    sp.dma_start(w2v[:, e], W2[e].rearrange("(k p) n -> p k n", p=P)).then_inc(s("w2_loaded"), 16)
            sp.wait_ge(s("flag_ready"), 1)
            slow = sp.value_load(flag_i[0:1, 0:1], min_val=0, max_val=1 << 30)

            def store_rows():
                with sp.Fori(0, NT) as i:
                    sp.wait_ge(s("x1_kept"), i + 1)
                    sp.wait_ge(s("rows_kept"), i + 1)
                    sp.dma_start(node_rows[bass.ds(i * P, P), :],
                                 X[:, bass.ds(i, 1), :].squeeze(1)).then_inc(s("rows_stored"), 16)
            with sp.If(slow == 0):
                after_ring()
                store_rows()
            with sp.Else():
                sp.wait_ge(s("lhs_ready"), 3)
                sp.dma_start(wide_iota, tab[:, T_COLS:]).then_inc(s("wide_loaded"), 16)

                def store_beta(i):
                    sp.wait_ge(s("beta_whole"), i + 1)
                    sp.dma_start(beta_rows[bass.ds(i * P, P), :], whole_beta).then_inc(s("beta_stored"), 16)
                with sp.Fori(0, NT) as i:
                    store_beta(i)
                sp.wait_ge(s("slow_x1"), NT)
                after_ring()
                store_rows()
            for e in range(W2_LATE):
                sp.dma_start(w2v[:, e], W2[e].rearrange("(k p) n -> p k n", p=P)).then_inc(s("w2_loaded"), 16)
            sp.wait_ge(s("y_stored"), 16 * TOKT)

        @block.gpsimd
        def _(pool):
            pool.dma_start(tabs[:, :], tab[:, 0:T_COLS]).then_inc(s("tables_loaded"), 16)
            pool.memset(raw[:, 0, 2 * P:3 * P], PAD_SRC)
            pool.memset(raw[:, 1, 2 * P:3 * P], PAD_DST).then_inc(s("edge_pads_set"), 1)
            pool.memset(onesb[:, :], 1.0)
            pool.memset(onesf[:, :], 1.0)
            pool.memset(eps[:, :], EPS)
            pool.memset(zero_col[:, :], 0.0)
            pool.memset(b2_stack[:, :], 0.0).then_inc(s("consts_ready"), 1)
            pool.dma_start(bias_b[:, :], bias.partition_broadcast(P)).then_inc(s("small_loaded"), 16)
            pool.dma_start(br_b[:, :], br.partition_broadcast(P)).then_inc(s("small_loaded"), 16)
            pool.dma_start(wr_sb[:, :, :], Wr.rearrange("(k p) n -> p k n", p=P)).then_inc(s("small_loaded"), 16)
            pool.dma_start(b1_rows[:, :], b1.rearrange("e (c p) -> (e c) p", p=P)).then_inc(s("small_loaded"), 16)
            pool.dma_start(b2_sb, b2).then_inc(s("small_loaded"), 16)
            def take_wait(took, col):
                pool.tensor_tensor(taker[:, col:col + 1], eps[:, :], eps[:, :], ALU.add).then_inc(took, 1)
            last_node, last_beta = pool.to_reg(N - 1), pool.to_reg(NS - 1)
            pool.wait_ge(s("small_loaded"), 80)
            with pool.Fori(0, NT) as i:
                pool.wait_ge(s("xn_ready"), i + 1)
                pool.tensor_tensor(X[:, bass.ds(i, 1), 0:H].squeeze(1), X[:, bass.ds(i, 1), 0:H].squeeze(1),
                                   bias_b[:, :], ALU.add).then_inc(s("bias_added"), 1)
            pool.wait_ge(s("b2_parts"), 3)
            pool.wait_ge(s("consts_ready"), 1)
            for a in range(3):
                pool.dma_start(b2_stack[a * NEXP:(a + 1) * NEXP, :], b2_part[:, a, :]).then_inc(s("b2_stacked"), 16)
            pool.wait_ge(s("flag_ready"), 1)
            slow = pool.value_load(flag_i[0:1, 0:1], min_val=0, max_val=1 << 30)
            with pool.If(slow == 0):
                pool.nop()
            with pool.Else():
                pool.wait_ge(s("beta_stored"), 16 * NT)
                pool.wait_ge(s("slow_lists"), 2)
                def gather(t, h):
                    wait_for(pool, s("edge_summed"), t + h * ETP)
                    pool.tensor_copy(gather_col[:, :], gather_at[:, bass.ds(t, 1)]).then_inc(s("col_ready"), 1)
                    wait_for(pool, s("took_slow"), t + h * ETP)
                    pool.wait_ge(s("col_ready"), t + (h * ETP + 1))
                    take_wait(s("took_slow"), 2)
                    pool.indirect_dma_start(got_row, None, beta_rows,
                                            bass.IndirectOffsetOnAxis(ap=gather_col[:, :], axis=0),
                                            bounds_check=last_beta, oob_is_err=False).then_inc(s("got_rows"), 16)
                for h in range(2):
                    gather(0, h)
                    with pool.Fori(1, ETP) as t:
                        gather(t, h)
            pool.nop()
            pool.wait_ge(s("rows_stored"), 16 * NT)
            pool.wait_ge(s("nodes_ready"), 1)
            for j in range(TOKT):
                pool.indirect_dma_start(rows[:, j, :], None, node_rows,
                                        bass.IndirectOffsetOnAxis(ap=node_i[:, j:j + 1], axis=0),
                                        bounds_check=last_beta, oob_is_err=False
                                        ).then_inc(rows_got[j] if j < AHEAD else s("later_rows"), 16)
            def store_result(j):
                wait_for(pool, s("took"), j)
                pool.wait_ge(s("y_ready"), j + 1)
                take_wait(s("took"), 1)
                pool.indirect_dma_start(out, bass.IndirectOffsetOnAxis(ap=row_at[:, :], axis=0), y_out, None,
                                        bounds_check=last_node, oob_is_err=False).then_inc(s("y_stored"), 16)
            store_result(0)
            with pool.Fori(1, TOKT) as j:
                store_result(j)

        @block.scalar
        def _(act):
            def bank_evac(c, q):
                nc.scalar.activation(chunk[:, :, q * QN:(q + 1) * QN],
                                     bankA[q][:, 0:QC].rearrange("p (d s) -> p s d", s=SB), ACT.Copy,
                                     accum_out=bank_sums[:, bass.ds(c * QB + q, 1)]).then_inc(s("bank_out"), 1)

            def turned_evac(c, k):
                n = min(TURN, SB - k * TURN) * P
                act.wait_ge(s("turned"), c * ROUNDS + (k + 1))
                nc.scalar.copy(adj[:, bass.ds(c, 1), k * TURN * P:k * TURN * P + n].squeeze(1),
                               bankR[:, 0:n]).then_inc(s("turned_out"), 1)

            def widen(i, par, d0=0, d1=NT):
                nc.scalar.copy(lhs[:, par, d0:d1, :], adj[:, d0:d1, bass.ds(i * P, P)]).then_inc(s("lhs_ready"), 1)

            def stairs(i, g, first):
                if not first:
                    act.wait_ge(s("tiles_done"), i * NG + (g + 1 - NG))
                for r in range(g * GRP, (g + 1) * GRP):
                    if r in ACT_TILES:
                        last = nc.scalar.activation(ring[:, r, 0:P], iota16[:, 0:P], ACT.Sign, scale=-1.0,
                                                    bias=lane_half[:, bass.ds(i * TPC + r, 1)])
                last.then_inc(s("stairs_ready"), 1)

            def root(i):
                act.wait_ge(s("var_ready"), i + 1)
                nc.scalar.activation(std[:, :], mv[:, 1:2], ACT.Sqrt, bias=eps[:, 0:1]).then_inc(s("std_ready"), 1)

            def xT_copy(i):
                act.wait_ge(s("xT_turned"), i + 1)
                nc.scalar.copy(xT[:, :], bankT[:, :]).then_inc(s("xT_ready"), 1)

            act.wait_ge(s("consts_ready"), 1)
            root(0)

            def body(i, first=False, final=False):
                def bank(q):
                    act.wait_ge(s("tiles_done"), i * NG + (CLOSE[(0, q)] // GRP + 1))
                    bank_evac(i, q)
                if first:
                    xT_copy(0)
                    act.wait_ge(s("iota_ready"), 2)
                    for g in range(4):
                        stairs(i, g, first)
                    root(1)
                else:
                    if not final:
                        root(i + 1)
                    act.wait_ge(s("alpha_done"), i)
                    xT_copy(i)
                    act.wait_ge(s("tiles_done"), i * NG + (CLOSE[(-1, QB - 1)] // GRP + 1))
                    bank_evac(i - 1, QB - 1)
                    for g in range(2, 6):
                        stairs(i, g, first)
                    turned_evac(i - 1, 0)
                act.wait_ge(s("beta_done"), i + 1)
                nc.scalar.copy(beta[:, 0, bass.ds(i, 1), :].squeeze(1), bankB[:, :]).then_inc(s("beta_hi"), 1)
                if first:
                    stairs(i, 4, first)
                    stairs(i, 5, first)
                stairs(i, 6, first)
                if not first:
                    turned_evac(i - 1, 1)
                stairs(i, 7, first)
                stairs(i, 8, first)
                stairs(i, 9, first)
                stairs(i, 10, first)
                if not first:
                    turned_evac(i - 1, 2)
                if final:
                    act.wait_ge(s("alpha_done"), NT)
                    act.wait_ge(s("turned_out"), ROUNDS * (NT - 1))
                    widen(0, 0, 0, NT - 1)
                bank(0)
                bank(1)
                if not final:
                    stairs(i + 1, 0, False)
                    stairs(i + 1, 1, False)
                bank(2)

            body(0, True)
            with act.Fori(1, NT - 1) as i:
                body(i)
            body(NT - 1, final=True)
            act.wait_ge(s("tiles_done"), NT * NG)
            bank_evac(NT - 1, QB - 1)
            turned_evac(NT - 1, 0)
            act.wait_ge(s("turned_out"), ROUNDS * (NT - 1) + 1)
            widen(0, 0, NT - 1, NT)
            turned_evac(NT - 1, 1)
            turned_evac(NT - 1, 2)
            widen(1, 1)

            def second_norm(i):
                act.wait_ge(s("var2_ready"), i + 1)
                nc.scalar.activation(std2[:, :], mv2[:, 1:2], ACT.Sqrt, bias=eps[:, 0:1]).then_inc(s("std2_ready"), 1)
                nc.scalar.copy(X[:, bass.ds(i, 1), 0:H].squeeze(1), part[:, :]).then_inc(s("x1_kept"), 1)
                act.wait_ge(s("xn2_turned"), i + 1)
                wait_for(act, s("logits_done"), i)
                nc.scalar.copy(xT[:, :], bankT[:, :]).then_inc(s("xT2_ready"), 1)

            act.wait_ge(s("flag_ready"), 1)
            slow = act.value_load(flag_i[0:1, 0:1], min_val=0, max_val=1 << 30)
            with act.If(slow == 0):
                def block_out(i, par, final=False):
                    if not final:
                        act.wait_ge(s("sums_done"), i + 1)
                        widen(i + 2, par)
                    second_norm(i)
                block_out(0, 0)
                block_out(1, 1)
                with act.Fori(1, NT // 2 - 1) as m:
                    for par in range(2):
                        block_out(m * 2 + par, par)
                block_out(NT - 2, 0, final=True)
                block_out(NT - 1, 1, final=True)
            with act.Else():
                second_norm(0)
                with act.Fori(1, NT) as i:
                    second_norm(i)
            act.nop()

            act.wait_ge(s("shift_ready"), 1)
            nc.scalar.activation(expo[:, :, :], shifted[:, :, :], ACT.Exp).then_inc(s("exp_ready"), 1)

            def xs_evac(j):
                act.wait_ge(s("xs_turned"), j + 1)
                nc.scalar.copy(xT[:, :], bankT[:, :]).then_inc(s("xs_out"), 1)

            def relu(j):
                act.wait_ge(s("h_turned"), j + 1)
                act.wait_ge(s("b1col_ready"), j + 1)
                for c in range(KC):
                    last = nc.scalar.activation(hidT[:, c * P:(c + 1) * P], bankC[:, c * P:(c + 1) * P], ACT.Relu,
                                                bias=b1_col[:, c:c + 1])
                last.then_inc(s("hT_ready"), 1)

            xs_evac(0)
            with act.Fori(0, TOKT - 1) as j:
                xs_evac(j + 1)
                relu(j)
            relu(TOKT - 1)

        @block.vector
        def _(dve):
            V = nc.vector
            ch = Chain(dve, s("dve_pre"))
            V.memset(X[96:P, NT - 1, 0:H], 0.0).then_inc(s("pad_rows_zero"), 1)
            dve.wait_ge(x_loaded[0], 16)
            V.bn_stats(stats[:, :], X[:, 0, 0:H]).then_inc(s("stats_ready"), 1)
            dve.wait_ge(s("stats_ready"), 1)
            V.bn_aggr(mv[:, :], stats[:, :]).then_inc(s("var_ready"), 1)
            dve.wait_ge(s("tables_loaded"), 16)
            V.tensor_copy(iota16[:, :], tabs[:, T_IOTA:T_IOTA + WC])
            V.tensor_copy(trib[:, :], tabs[:, T_TRI:T_TRI + P])
            V.tensor_copy(pay[:, :, :], tabs[:, T_PAY:T_PAY + NT * NPAY].rearrange("p (i v) -> p i v", i=NT))
            V.tensor_copy(diff[:, :], tabs[:, T_DIFF:T_DIFF + P]).then_inc(s("iota_ready"), 1)
            dve.wait_ge(s("std_ready"), 1)
            V.reciprocal(rstd[:, :], std[:, :]).then_inc(s("rstd_ready"), 1)
            dve.wait_ge(s("rstd_ready"), 1)
            V.tensor_scalar(xn[:, :], X[:, 0, 0:H], mv[:, 0:1], rstd[:, :], ALU.subtract,
                            ALU.mult).then_inc(s("xn_ready"), 1)
            dve.wait_ge(s("edges_loaded"), 16 * 8)
            V.tensor_copy(rawf, raw).then_inc(s("edges_float"), 1)
            dve.wait_ge(s("edges_turned"), 1)
            ch.link(V.tensor_copy(src_i, bankA[0][:, 0:ETP]))
            V.tensor_copy(dst_f, bankA[1][:, 0:ETP]).then_inc(s("edges_turned_out"), 1)
            V.tensor_scalar(lane, src_i, P - 1, None, ALU.bitwise_and)
            ch.link(V.tensor_scalar(block_i, src_i, 7, None, ALU.arith_shift_right))
            V.tensor_copy(lane_f, lane)
            V.tensor_scalar(lane_half[:, :], lane, 0.5, None, ALU.add)
            dve.wait_ge(s("edges_turned_out"), 1)
            ch.link(V.scalar_tensor_tensor(key, dst_f, float(SB), block_i, ALU.mult, ALU.add))
            V.tensor_tensor(key, key, tabs[:, T_BASE:T_BASE + ETP], ALU.subtract).then_inc(s("iota_ready"), 1)
            dve.wait_ge(s("iota_ready"), 2)

            def add_alpha(i):
                dve.wait_ge(s("alpha_done"), i + 1)
                dve.wait_ge(s("bias_added"), i + 1)
                V.tensor_tensor(X[:, bass.ds(i, 1), 0:H].squeeze(1), X[:, bass.ds(i, 1), 0:H].squeeze(1),
                                bankC[:, :], ALU.add).then_inc(s("alpha_added"), 1)

            def body(i, first=False, final=False):
                for g in range(NG):
                    if not first:
                        dve.wait_ge(s("tiles_done"), i * NG + (g + 1 - NG))
                    if g == 2 and not final:
                        dve.wait_ge(s("stats_ready"), i + 2)
                        dve.wait_ge(s("xn_ready"), i + 1)
                    for r in range(g * GRP, (g + 1) * GRP):
                        if r not in ACT_TILES:
                            V.tensor_scalar(ring[:, r, 0:P], iota16[:, 0:P], lane_f[:, bass.ds(i * TPC + r, 1)], 0.5,
                                            ALU.is_le, ALU.subtract)
                        last = V.tensor_scalar(ring[:, r, P:OH], iota16[:, :], key[:, bass.ds(i * TPC + r, 1)],
                                               1.0 if r in ACT_TILES else 2.0, ALU.is_equal, ALU.mult)
                    last.then_inc(s("hot_ready"), 1)
                    if g == 1:
                        if not first:
                            add_alpha(i - 1)
                        else:
                            dve.wait_ge(x_loaded[1], 16)
                        if not final:
                            V.bn_stats(stats[:, :], X[:, bass.ds(i + 1, 1), 0:H].squeeze(1)).then_inc(s("stats_ready"), 1)
                    if g == 2 and not final:
                        V.bn_aggr(mv[:, :], stats[:, :]).then_inc(s("var_ready"), 1)
                    if g == 3 and not final:
                        dve.wait_ge(s("std_ready"), i + 2)
                        V.reciprocal(rstd[:, :], std[:, :]).then_inc(s("rstd_ready"), 1)
                    if g == 4 and not final:
                        dve.wait_ge(s("rstd_ready"), i + 2)
                        dve.wait_ge(s("xT_turned"), i + 1)
                        V.tensor_scalar(xn[:, :], X[:, bass.ds(i + 1, 1), 0:H].squeeze(1), mv[:, 0:1], rstd[:, :],
                                        ALU.subtract, ALU.mult).then_inc(s("xn_ready"), 1)
                    if g == 9:
                        dve.wait_ge(s("beta_hi"), i + 1)
                        V.tensor_tensor(beta[:, 1, bass.ds(i, 1), :].squeeze(1), bankB[:, :],
                                        beta[:, 0, bass.ds(i, 1), :].squeeze(1), ALU.subtract).then_inc(s("beta_rest"), 1)

            body(0, first=True)
            ch.link(V.tensor_scalar(missed, key, float(WC), None, ALU.is_ge))
            ch.link(V.scalar_tensor_tensor(missed, key, 0.0, missed, ALU.is_lt, ALU.add))
            for i in range(2, NT):
                dve.wait_ge(x_loaded[i], 16)
            V.tensor_reduce(checks[:, 0:1], missed, AX, ALU.add).then_inc(s("iota_ready"), 1)
            with dve.Fori(1, NT - 1) as i:
                body(i)
            body(NT - 1, final=True)
            add_alpha(NT - 1)

            dve.wait_ge(s("small_loaded"), 80)
            V.tensor_copy(b2_part[:, 0, :], b2_sb).then_inc(s("b2_parts"), 1)
            dve.wait_ge(s("b2_parts"), 1)
            ch.link(V.tensor_tensor(b2_rest, b2_sb, b2_part[:, 0, :], ALU.subtract))
            V.tensor_copy(b2_part[:, 1, :], b2_rest).then_inc(s("b2_parts"), 1)
            dve.wait_ge(s("b2_parts"), 2)
            V.tensor_tensor(b2_part[:, 2, :], b2_rest, b2_part[:, 1, :], ALU.subtract).then_inc(s("b2_parts"), 1)

            dve.wait_ge(s("bank_out"), NT * QB)
            ch.link(V.tensor_reduce(count[:, :], bank_sums[:, :], AX, ALU.max))
            V.tensor_scalar(checks[:, 1:2], count[:, :], float(ADJ_EXACT), None, ALU.is_ge).then_inc(s("sums_checked"), 1)
            dve.wait_ge(s("checks_summed"), 1)
            ch.link(V.tensor_reduce(flag_f[:, :], bankB[:, 0:2], AX, ALU.add))
            V.tensor_scalar(flag_i[:, :], flag_f[:, :], float(N_PAD_EDGES), None, ALU.subtract).then_inc(s("flag_ready"), 1)
            dve.wait_ge(s("b1_turned"), 1)
            V.tensor_copy(b1T[:, :], bankC[:, 0:NEXP * KC]).then_inc(s("b1_ready"), 1)

            def second_norm(i, ch):
                ch.link(V.bn_stats(stat2[:, :], part[:, :]))
                V.tensor_copy(taker[:, 0:1], stat2[:, 0:1])
                V.bn_aggr(mv2[:, 0:2], stat2[:, :]).then_inc(s("var2_ready"), 1)
                dve.wait_ge(s("std2_ready"), i + 1)
                ch.link(V.reciprocal(mv2[:, 1:2], std2[:, :]))
                wait_for(dve, s("xn2_turned"), i)
                V.tensor_scalar(xn[:, :], part[:, :], mv2[:, 0:1], mv2[:, 1:2], ALU.subtract, ALU.mult).then_inc(s("xn2_ready"), 1)
                V.tensor_copy(X[:, bass.ds(i, 1), H:H + 2].squeeze(1), mv2[:, :]).then_inc(s("rows_kept"), 1)

            dve.wait_ge(s("flag_ready"), 1)
            slow = dve.value_load(flag_i[0:1, 0:1], min_val=0, max_val=1 << 30)
            with dve.If(slow == 0):
                def graph_out(i, par):
                    c = Chain(dve, s("dve_fast"), i * 4)
                    Xi = X[:, bass.ds(i, 1), 0:H].squeeze(1)
                    dve.wait_ge(s("sums_done"), i + 1)
                    c.link(V.tensor_tensor(count[:, :], bankA[2 + par][:, 0:1], padding[:, bass.ds(i, 1)], ALU.add))
                    c.link(V.reciprocal(rcount[:, :], count[:, :]))
                    wait_for(dve, s("x1_kept"), i)
                    V.scalar_tensor_tensor(part[:, :], bankA[par][:, :], rcount[:, 0:1], Xi, ALU.mult, ALU.add).then_inc(s("x1_ready"), 1)
                    dve.wait_ge(s("x1_ready"), i + 1)
                    second_norm(i, c)
                    assert c.n == 4
                graph_out(0, 0)
                graph_out(1, 1)
                with dve.Fori(1, NT // 2) as m:
                    for par in range(2):
                        graph_out(m * 2 + par, par)
            with dve.Else():
                dve.wait_ge(s("lhs_ready"), 3)
                def rejoin(i):
                    wait_for(dve, s("beta_stored"), i * 16)
                    V.tensor_tensor(whole_beta, beta[:, 0, bass.ds(i, 1), :].squeeze(1),
                                    beta[:, 1, bass.ds(i, 1), :].squeeze(1), ALU.add).then_inc(s("beta_whole"), 1)
                rejoin(0)
                with dve.Fori(1, NT) as i:
                    rejoin(i)
                V.tensor_scalar(gather_at, dst_f, float(NS - 1), None, ALU.min).then_inc(s("slow_lists"), 1)
                dve.wait_ge(s("wide_loaded"), 16)
                for h in range(2):
                    V.tensor_scalar(src_rel, src_i, float(h * T_WIDE), None, ALU.subtract).then_inc(s("slow_lists"), 1)
                    dve.wait_ge(s("slow_lists"), 2 + h)
                    def wide(t):
                        wait_for(dve, s("edge_summed"), t + h * ETP)
                        V.tensor_scalar(wide_hot, wide_iota, src_rel[:, bass.ds(t, 1)], None,
                                        ALU.is_equal).then_inc(s("wide_ready"), 1)
                    wide(0)
                    with dve.Fori(1, ETP) as t:
                        wide(t)
                    dve.wait_ge(s("edge_summed"), (h + 1) * ETP)
                    c = Chain(dve, s("dve_slow"), 2 * HB * h)
                    sums = [bankA[0], bankA[1], bankA[2], bankA[3], bankT]
                    for b in range(HB):
                        i = h * HB + b
                        c.link(V.tensor_tensor(count[:, :], bankB[:, b:b + 1], padding[:, i:i + 1], ALU.add))
                        c.link(V.reciprocal(rcount[:, :], count[:, :]))
                        V.scalar_tensor_tensor(X[:, i, 0:H], sums[b][:, :], rcount[:, 0:1], X[:, i, 0:H],
                                               ALU.mult, ALU.add).then_inc(s("slow_x1"), 1)
                dve.wait_ge(s("slow_x1"), NT)
                def block_norm(i):
                    wait_for(dve, s("x1_kept"), i)
                    wait_for(dve, s("xn2_ready"), i)
                    V.tensor_copy(part[:, :], X[:, bass.ds(i, 1), 0:H].squeeze(1)).then_inc(s("x1_ready"), 1)
                    dve.wait_ge(s("x1_ready"), i + 1)
                    second_norm(i, Chain(dve, s("dve_slow"), 4 * HB + i * 2))
                block_norm(0)
                with dve.Fori(1, NT) as i:
                    block_norm(i)
            dve.nop()

            ch = Chain(dve, s("dve_route"))
            dve.wait_ge(s("logits_done"), NT)
            full = [P, NT, NEXP]

            def over_exp(ap):
                return ap.unsqueeze(2).broadcast_to(full)

            def over_tiles(ap):
                return ap.unsqueeze(1).broadcast_to(full)
            logits = bankB[:, 0:NT * NEXP].rearrange("p (i e) -> p i e", e=NEXP)
            ch.link(V.tensor_tensor(logit[:, :, :], logits, over_tiles(br_b[:, :]), ALU.add))
            ch.link(V.tensor_reduce(top[:, :], logit[:, :, :], AX, ALU.max))
            V.tensor_tensor(shifted[:, :, :], logit[:, :, :], over_exp(top[:, :]), ALU.subtract).then_inc(s("shift_ready"), 1)
            ch.link(V.tensor_tensor(eqmax[:, :, :], logit[:, :, :], over_exp(top[:, :]), ALU.is_equal))
            ch.link(V.scalar_tensor_tensor(place[:, :, :], eqmax[:, :, :], -float(NEXP - 1), not_top, ALU.mult, ALU.add))
            ch.link(V.tensor_reduce(best[:, :], place[:, :, :], AX, ALU.min))
            V.tensor_tensor(hot[:, :, :], over_tiles(iota8), over_exp(best[:, :]), ALU.is_equal).then_inc(s("chosen"), 1)
            dve.wait_ge(s("exp_ready"), 1)
            ch.link(V.tensor_reduce(esum[:, :], expo[:, :, :], AX, ALU.add))
            ch.link(V.reciprocal(gate[:, :], esum[:, :]))
            ch.link(V.tensor_copy(pay[:, :, 3], gate[:, :]))
            dve.wait_ge(s("ranked"), 1)
            ch.link(V.tensor_scalar(n_exp[:, :], bankC[:, P:P + NEXP], float(P - 1), None, ALU.add))
            ch.link(V.tensor_scalar(t_exp[:, :], n_exp[:, :], 7, None, ALU.arith_shift_right))
            ch.link(V.tensor_copy(tiles_f[:, :], t_exp[:, :]))
            ch.link(V.tensor_tensor(before[:, :, :], tri8, tiles_f[:, :].unsqueeze(1).broadcast_to([P, NEXP, NEXP]), ALU.mult))
            ch.link(V.tensor_reduce(first_slot[:, :], before[:, :, :], AX, ALU.add))
            ch.link(V.scalar_tensor_tensor(place[:, :, :], over_tiles(first_slot[:, :]), float(P),
                                           bankC[:, 0:NT * NEXP].rearrange("p (i e) -> p i e", e=NEXP), ALU.mult, ALU.add))
            ch.link(V.tensor_tensor(place[:, :, :], place[:, :, :], hot[:, :, :], ALU.mult))
            ch.link(V.tensor_reduce(slot_f[:, :], place[:, :, :], AX, ALU.add))
            ch.link(V.scalar_tensor_tensor(slot_i[:, :], padding, float(2 * SLOTS), slot_f[:, :], ALU.mult, ALU.add))
            ch.link(V.tensor_tensor(gate_rest[:, :], gate[:, :], pay[:, :, 3], ALU.subtract))
            ch.link(V.tensor_copy(pay[:, :, 4], gate_rest[:, :]))
            ch.link(V.tensor_tensor(pay[:, :, 5], gate_rest[:, :], pay[:, :, 4], ALU.subtract))
            V.tensor_scalar(slot_lane[:, :], slot_i[:, :], P - 1, None, ALU.bitwise_and)
            ch.link(V.tensor_scalar(slot_tile[:, :], slot_i[:, :], 7, None, ALU.arith_shift_right))
            V.tensor_copy(slot_lane_f[:, :], slot_lane[:, :])
            ch.link(V.tensor_copy(slot_tile_f[:, :], slot_tile[:, :]))
            sh = [P, NT, TOKT]
            V.tensor_tensor(tile_hot[:, :, :], tabs[:, T_IOTA:T_IOTA + TOKT].unsqueeze(1).broadcast_to(sh),
                            slot_tile_f[:, :].unsqueeze(2).broadcast_to(sh), ALU.is_equal)
            for i in range(NT):
                last = V.tensor_scalar(lane_hot[:, i, :], iota16[:, 0:P], slot_lane_f[:, i:i + 1], None, ALU.is_equal)
            ch.link(last)
            sh = [P, NT, NPAY, TOKT]
            V.tensor_tensor(sent[:, :, :, :], tile_hot[:, :, :].unsqueeze(2).broadcast_to(sh),
                            pay[:, :, :].unsqueeze(3).broadcast_to(sh), ALU.mult).then_inc(s("sent_ready"), 1)
            dve.wait_ge(s("at_slots"), 1)
            ch.link(V.tensor_copy(got[:, :, :], bankC[:, 2 * P:2 * P + NPAY * TOKT].rearrange("p (v j) -> p v j", v=NPAY)))
            ch.link(V.scalar_tensor_tensor(node_f[:, :], got[:, 0, :], float(P), got[:, 1, :], ALU.mult, ALU.add))
            V.tensor_copy(node_i[:, :], node_f[:, :]).then_inc(s("nodes_ready"), 1)
            ch.link(V.scalar_tensor_tensor(out_f[:, :], got[:, 2, :], -float(SLOTS), node_f[:, :], ALU.mult, ALU.add))
            V.tensor_scalar(out_i[:, :], out_f[:, :], float(SLOTS), None, ALU.add)
            ch.link(V.tensor_tensor(gate_s[:, :], got[:, 3, :], got[:, 4, :], ALU.add))
            ch.link(V.tensor_tensor(gate_s[:, :], gate_s[:, :], got[:, 5, :], ALU.add))
            ft = [P, TOKT, NEXP]
            ch.link(V.tensor_tensor(tiles_to[:, :], first_slot[:, :], tiles_f[:, :], ALU.add))
            ch.link(V.tensor_tensor(past[:, :, :], tabs[:, T_IOTA:T_IOTA + TOKT].unsqueeze(2).broadcast_to(ft),
                                    tiles_to[:, :].unsqueeze(1).broadcast_to(ft), ALU.is_ge))
            ch.link(V.tensor_reduce(exp_f[:, :], past[:, :, :], AX, ALU.add))
            ch.link(V.tensor_scalar(exp_f[:, :], exp_f[:, :], float(NEXP - 1), None, ALU.min))
            V.tensor_copy(exp_i[:, :], exp_f[:, :]).then_inc(s("experts_ready"), 1)
            ch.link(V.tensor_tensor(exp_hot[:, :, :], iota8.unsqueeze(1).broadcast_to(ft),
                                    exp_f[:, :].unsqueeze(2).broadcast_to(ft), ALU.is_equal))
            dve.wait_ge(s("b1_ready"), 1)
            b1v = b1T[:, :].rearrange("p (e c) -> p c e", c=KC)
            assert TOKT * NEXP <= H
            for c in range(KC):
                prod = (bias_b, part)[c % 2][:, 0:TOKT * NEXP].rearrange("p (j e) -> p j e", e=NEXP)
                ch.link(V.tensor_tensor(prod, exp_hot[:, :, :], b1v[:, c:c + 1, :].broadcast_to(ft), ALU.mult))
                last = V.tensor_reduce(b1_sel[:, :, c:c + 1].squeeze(2), prod, AX, ALU.add)
            ch.link(last)

            def xs_norm(j):
                wait_for(dve, s("xs_turned"), j)
                r = rows[:, bass.ds(j, 1), :].squeeze(1)
                V.tensor_scalar(xn[:, :], r[:, 0:H], r[:, H:H + 1], r[:, H + 1:H + 2], ALU.subtract,
                                ALU.mult).then_inc(s("xs_ready"), 1)

            def h_evac(j):
                dve.wait_ge(s("h_done"), j + 1)
                V.tensor_copy(hid, bankB[:, :]).then_inc(s("h_out"), 1)
                wait_for(dve, s("hT_ready"), j)
                V.tensor_copy(b1_col[:, :], b1_sel[:, bass.ds(j, 1), :].squeeze(1)).then_inc(s("b1col_ready"), 1)

            def result(j):
                dve.wait_ge(s("y_done"), j + 1)
                wait_for(dve, s("y_stored"), j * 16)
                r = rows[:, bass.ds(j, 1), :].squeeze(1)
                V.tensor_copy(row_at[:, :], out_i[:, bass.ds(j, 1)])
                V.scalar_tensor_tensor(y_out, bankA[0][:, :], gate_s[:, bass.ds(j, 1)], r[:, 0:H], ALU.mult,
                                       ALU.add).then_inc(s("y_ready"), 1)

            dve.wait_ge(rows_got[0], 16)
            xs_norm(0)
            V.tensor_scalar(pick[:, :, :], exp_f[:, :].unsqueeze(2).broadcast_to([P, TOKT, P]),
                            tabs[:, T_KMOD:T_KMOD + 1], None, ALU.is_equal).then_inc(s("pick_ready"), 1)
            dve.wait_ge(rows_got[1], 16)
            xs_norm(1)
            h_evac(0)

            def step(j):
                xs_norm(j + 1)
                h_evac(j)
                result(j - 1)
            for j in range(1, AHEAD - 1):
                dve.wait_ge(rows_got[j + 1], 16)
                step(j)
            dve.wait_ge(s("later_rows"), 16 * (TOKT - AHEAD))
            with dve.Fori(AHEAD - 1, TOKT - 1) as j:
                step(j)
            h_evac(TOKT - 1)
            result(TOKT - 2)
            result(TOKT - 1)

        @block.tensor
        def _(pe):
            mm = nc.tensor.matmul
            def turn_edges():
                pe.wait_ge(s("edges_float"), 1)
                for a in range(2):
                    for c in range(3):
                        last = nc.tensor.transpose(bankA[a][:, c * P:(c + 1) * P], rawf[:, a, c * P:(c + 1) * P], ident)
                last.then_inc(s("edges_turned"), 1)

            def turn(c, k):
                pe.wait_ge(s("bank_out"), (c + 1) * QB)
                wait_for(pe, s("turned_out"), c * ROUNDS + k)
                for b in range(k * TURN, min((k + 1) * TURN, SB)):
                    at = (b - k * TURN) * P
                    last = mm(bankR[:, at:at + P], chunk[:, b, :], diff[:, :], start=True, stop=True)
                last.then_inc(s("turned"), 1)

            def tiles(i, g, first, final):
                pe.wait_ge(s("hot_ready"), i * NG + (g + 1))
                pe.wait_ge(s("stairs_ready"), i * NG + (g + 1))
                for r in range(g * GRP, (g + 1) * GRP):
                    for c, q, k0, n, col in segments(r):
                        if (c < 0 and first) or (c > 0 and final):
                            continue
                        start = OPEN[(c, q)] == r and c >= 0 and not (c == 0 and (1, q) in OPEN and not first)
                        if start:
                            if c == 1:
                                pe.wait_ge(s("bank_out"), i * QB + (q + 1))
                            elif not first:
                                pe.wait_ge(s("bank_out"), i * QB + (q + 1 - QB))
                        last = mm(bankA[q][:, col:col + n], ring[:, r, 0:P], ring[:, r, P + k0:P + k0 + n],
                                  start=start, stop=True, skip_group_check=True)
                last.then_inc(s("tiles_done"), 1)

            def body(i, first=False, final=False):
                pe.wait_ge(s("xn_ready"), i + 1)
                for c in range(KC):
                    last = nc.tensor.transpose(bankT[:, c * P:(c + 1) * P], xn[:, c * P:(c + 1) * P], ident)
                last.then_inc(s("xT_turned"), 1)
                if not first:
                    tiles(i, 0, first, final)
                    tiles(i, 1, first, final)
                if first:
                    turn_edges()
                pe.wait_ge(s("xT_ready"), i + 1)
                if first:
                    pe.wait_ge(s("wn_loaded"), 16)
                else:
                    pe.wait_ge(s("beta_rest"), i)
                for c in range(KC):
                    last = mm(bankB[:, :], xT[:, c * P:(c + 1) * P], wn_sb[:, c, :], start=c == 0, stop=c == KC - 1)
                last.then_inc(s("beta_done"), 1)
                if not first:
                    turn(i - 1, 0)
                    tiles(i, 2, first, final)
                    tiles(i, 3, first, final)
                    turn(i - 1, 1)
                    pe.wait_ge(s("alpha_added"), i)
                else:
                    pe.wait_ge(s("wc_loaded"), 16)
                for c in range(KC):
                    last = mm(bankC[:, :], xT[:, c * P:(c + 1) * P], wc_sb[:, c, :], start=c == 0, stop=c == KC - 1)
                last.then_inc(s("alpha_done"), 1)
                if not first:
                    turn(i - 1, 2)
                else:
                    pe.wait_ge(s("edges_turned_out"), 1)
                    for g in range(4):
                        tiles(i, g, first, final)
                for g in range(4, NG):
                    tiles(i, g, first, final)

            body(0, first=True)
            body(1)
            with pe.Fori(2, NT - 1) as i:
                body(i)
            body(NT - 1, final=True)
            pe.wait_ge(s("alpha_added"), NT)
            pe.wait_ge(s("small_loaded"), 80)
            nc.tensor.transpose(bankC[:, 0:NEXP * KC], b1_rows[:, :], ident[0:NEXP * KC, 0:NEXP * KC]).then_inc(s("b1_turned"), 1)
            def partial(d, par=0):
                for a in range(2):
                    last = mm(bankA[par][:, :], lhs[:, par, d, :], beta[:, a, d, :], start=d == 0 and a == 0,
                              stop=True, skip_group_check=True)
                return last
            pe.wait_ge(s("lhs_ready"), 1)
            pe.wait_ge(s("bank_out"), NT * QB - QB + 1)
            partial(0)
            partial(1)
            turn(NT - 1, 0)
            for d in range(2, 5):
                partial(d)
            turn(NT - 1, 1)
            pe.wait_ge(s("sums_checked"), 1)
            pe.wait_ge(s("beta_rest"), NT)
            mm(bankB[:, 0:2], onesf[:, :], checks[:, :], start=True, stop=True).then_inc(s("checks_summed"), 1)
            partial(5)
            partial(6)
            turn(NT - 1, 2)
            partial(7)
            partial(8)
            pe.wait_ge(s("turned_out"), ROUNDS * NT)

            def second_turn(i):
                pe.wait_ge(s("xn2_ready"), i + 1)
                for c in range(KC):
                    last = nc.tensor.transpose(bankT[:, c * P:(c + 1) * P], xn[:, c * P:(c + 1) * P], ident)
                last.then_inc(s("xn2_turned"), 1)

            def router(i):
                pe.wait_ge(s("xT2_ready"), i + 1)
                for c in range(KC):
                    last = mm(bankB[:, bass.ds(i * NEXP, NEXP)], xT[:, c * P:(c + 1) * P], wr_sb[:, c, :],
                              start=c == 0, stop=c == KC - 1)
                last.then_inc(s("logits_done"), 1)

            pe.wait_ge(s("beta_rest"), NT)
            pe.wait_ge(s("flag_ready"), 1)
            slow = pe.value_load(flag_i[0:1, 0:1], min_val=0, max_val=1 << 30)
            with pe.If(slow == 0):
                def sums(i, par, first=False):
                    for d in range(NT):
                        mm(bankA[2 + par][:, 0:1], adj[:, d, bass.ds(i * P, P)], onesb[:, 0:1], start=d == 0, stop=d == NT - 1,
                           skip_group_check=True)
                    pe.wait_ge(s("lhs_ready"), i + 2)
                    for d in range(NT - 1 if first else 0, NT):
                        last = partial(d, par)
                        if d == HB and not first:
                            second_turn(i - 1)
                    last.then_inc(s("sums_done"), 1)
                    if not first:
                        router(i - 1)
                sums(0, 0, first=True)
                sums(1, 1)
                with pe.Fori(1, NT // 2) as m:
                    for par in range(2):
                        pe.wait_ge(s("x1_ready"), m * 2 + (par - 1))
                        sums(m * 2 + par, par)
                second_turn(NT - 1)
                router(NT - 1)
            with pe.Else():
                acc = [bankA[0], bankA[1], bankA[2], bankA[3], bankT]

                def edge(t, first=False):
                    pe.wait_ge(s("got_rows"), (t + 1) * 16)
                    pe.wait_ge(s("wide_ready"), t + 1)
                    for b in range(HB):
                        hot_b = wide_hot[:, b * P:(b + 1) * P]
                        mm(acc[b][:, :], hot_b, got_row, start=first, stop=True, skip_group_check=True)
                        last = mm(bankB[:, b:b + 1], hot_b, onesf[:, 0:1], start=first and b == 0, stop=True,
                                  skip_group_check=True)
                    last.then_inc(s("edge_summed"), 1)
                for h in range(2):
                    if h:
                        pe.wait_ge(s("slow_x1"), HB)
                    edge(h * ETP, first=True)
                    with pe.Fori(1, ETP) as t:
                        edge(t + h * ETP)
                pe.wait_ge(s("slow_x1"), NT)
                with pe.Fori(0, NT) as i:
                    second_turn(i)
                    router(i)
            pe.nop()

            pe.wait_ge(s("chosen"), 1)
            hv = hot[:, :, :].rearrange("p i e -> p (i e)")
            W = NT * NEXP
            mm(bankC[:, 0:W], trib[:, :], hv, start=True, stop=True, skip_group_check=True)
            for k in range(1, NT):
                mm(bankC[:, k * NEXP:W], onesb[:, :], hv[:, 0:W - k * NEXP], start=False, stop=True,
                   skip_group_check=True)
            for k in range(NT):
                last = mm(bankC[:, P:P + NEXP], onesb[:, :], hv[:, k * NEXP:(k + 1) * NEXP], start=False, stop=True,
                          skip_group_check=True)
            last.then_inc(s("ranked"), 1)

            pe.wait_ge(s("sent_ready"), 1)
            for i in range(NT):
                last = mm(bankC[:, 2 * P:2 * P + NPAY * TOKT], lane_hot[:, i, :],
                          sent[:, i, :, :].rearrange("p v j -> p (v j)"), start=i == 0, stop=i == NT - 1)
            last.then_inc(s("at_slots"), 1)

            def xs_turn(j):
                pe.wait_ge(s("xs_ready"), j + 1)
                for c in range(KC):
                    last = nc.tensor.transpose(bankT[:, c * P:(c + 1) * P], xn[:, c * P:(c + 1) * P], ident)
                last.then_inc(s("xs_turned"), 1)

            def expert_of(j):
                return pe.value_load(exp_i[0:1, bass.ds(j, 1)], min_val=0, max_val=NEXP - 1)

            def up(j):
                e = expert_of(j)
                pe.wait_ge(s("xs_out"), j + 1)
                for c in range(KC):
                    last = mm(bankB[:, :], xT[:, c * P:(c + 1) * P], w1_sb[:, bass.ds(e * (KC * H) + c * H, H)],
                              start=c == 0, stop=c == KC - 1)
                last.then_inc(s("h_done"), 1)

            def down(j):
                e = expert_of(j)
                pe.wait_ge(s("hT_ready"), j + 1)
                wait_for(pe, s("y_ready"), j)
                mm(bankA[0][:, :], pick[:, bass.ds(j, 1), :].squeeze(1), b2_stack[:, :], start=True, stop=False)
                for c in range(KC):
                    last = mm(bankA[0][:, :], hidT[:, c * P:(c + 1) * P], w2_sb[:, bass.ds(e * (KC * H) + c * H, H)],
                              start=False, stop=c == KC - 1)
                last.then_inc(s("y_done"), 1)

            def h_turn(j):
                pe.wait_ge(s("h_out"), j + 1)
                for c in range(KC):
                    last = nc.tensor.transpose(bankC[:, c * P:(c + 1) * P], hid[:, c * P:(c + 1) * P], ident)
                last.then_inc(s("h_turned"), 1)

            pe.wait_ge(s("experts_ready"), 1)
            xs_turn(0)
            pe.wait_ge(s("w1_loaded"), 16 * NEXP)
            up(0)
            xs_turn(1)
            h_turn(0)
            pe.wait_ge(s("pick_ready"), 1)
            pe.wait_ge(s("b2_stacked"), 48)
            up(1)
            xs_turn(2)
            pe.wait_ge(s("w2_loaded"), 16 * NEXP)
            down(0)
            h_turn(1)
            with pe.Fori(2, TOKT - 1) as j:
                up(j)
                xs_turn(j + 1)
                down(j - 1)
                h_turn(j)
            up(TOKT - 1)
            down(TOKT - 2)
            h_turn(TOKT - 1)
            down(TOKT - 1)


_INS = ['x', 'src', 'dst', 'L0_gnn_wc', 'L0_gnn_wn', 'L0_gnn_bias', 'L0_ffn_Wr', 'L0_ffn_br', 'L0_ffn_W1', 'L0_ffn_b1',
        'L0_ffn_W2', 'L0_ffn_b2']


def kernel(**inputs):
    import concourse.bacc as _bacc
    from concourse.bass_utils import run_bass_kernel_spmd as _run

    nc = _bacc.Bacc("TRN2", target_bir_lowering=False, num_devices=1, dynamic_dma_scratch_size=8192)
    arrays, args = {}, []
    for name in _INS:
        a = np.ascontiguousarray(inputs[name])
        arrays[f"in_{name}"] = a
        args.append(nc.dram_tensor(f"in_{name}", a.shape, mybir.dt.from_np(a.dtype), kind="ExternalInput").ap())
    t = tables()
    arrays["tables"] = t
    args.append(nc.dram_tensor("tables", t.shape, mybir.dt.float32, kind="ExternalInput").ap())
    args.append(nc.dram_tensor("result", (N, H), mybir.dt.float32, kind="ExternalOutput").ap())
    build(nc, *args)
    r = _run(nc, [arrays], core_ids=[0])
    return r.results[0]["result"]
```

```python
import numpy as np
import concourse.bass as bass
from concourse import mybir
from contextlib import ExitStack

P = 128
H = 512
KC = H // P
N = 1250
E_EDGES = 41250
NEXP = 8
NT = -(-N // P)
LAST = N - (NT - 1) * P
NS = NT * P
TPC = 33
ETP = NT * TPC
GRP = 3
NG = TPC // GRP
SB = NT
MARGIN = 12
WIN = 28
WC = WIN * SB
QN = 32
QB = P // QN
QC = QN * SB
ROW = H + 2
TOKT = (N - NEXP) // P + NEXP
SLOTS = TOKT * P
PAD_SRC, PAD_DST = 16384, 8192
N_PAD_EDGES = ETP * P - E_EDGES
EPS = 1e-5
HB = NT // 2
TURN = 4
ROUNDS = -(-SB // TURN)
NPAY = 6
POOL_HOTS = 3
AHEAD = 4
ADJ_EXACT = 2048
ACT_TILES = [r for r in range(TPC) if (r + 1) * 20 // TPC > r * 20 // TPC]
ACT_TILES_0 = [r for r in range(TPC) if r % 8]
BASE = [P * r // TPC - MARGIN for r in range(TPC)]


def segments(r):
    out, d = [], BASE[r]
    while d < BASE[r] + WIN:
        c, q = d // P, d % P // QN
        end = min(BASE[r] + WIN, (d // QN + 1) * QN)
        out.append((c, q, (d - BASE[r]) * SB, (end - d) * SB, d % QN * SB))
        d = end
    return out


OPEN = {}
CLOSE = {}
for _r in range(TPC):
    for _c, _q, _, _, _ in segments(_r):
        OPEN.setdefault((_c, _q), _r)
        CLOSE[(_c, _q)] = _r

T_ID = 0
T_TRI = T_ID + P
T_IOTA = T_TRI + P
T_BASE = T_IOTA + WC
T_PAD = T_BASE + ETP
T_PAY = T_PAD + NT
T_PLACE = T_PAY + NT * NPAY
T_DIFF = T_PLACE + NT * NEXP
T_TRI8 = T_DIFF + P
T_COLS = T_TRI8 + NEXP * NEXP
T_WIDE = HB * P


def tables():
    t = np.zeros((P, T_COLS + T_WIDE), np.float32)
    p = np.arange(P)
    t[:, T_ID:T_ID + P] = np.eye(P)
    t[:, T_TRI:T_TRI + P] = p[:, None] < p[None, :]
    t[:, T_IOTA:T_IOTA + WC] = np.arange(WC)
    t[:, T_BASE:T_BASE + ETP] = [SB * (P * i + b) for i in range(NT) for b in BASE]
    tok = P * np.arange(NT)[None, :] + p[:, None]
    t[:, T_PAD:T_PAD + NT] = tok >= N
    pay = np.zeros((P, NT, NPAY))
    pay[:, :, 0], pay[:, :, 1], pay[:, :, 2] = (tok - tok % P) * (tok < N), p[:, None] * (tok < N), tok < N
    t[:, T_PAY:T_PAY + NT * NPAY] = pay.reshape(P, -1)
    t[:, T_PLACE:T_DIFF] = (np.arange(NEXP) + NEXP - 1 + 8 * NEXP * (tok >= N)[:, :, None]).reshape(P, -1)
    d = np.eye(P) / 2 - np.eye(P, k=-1) / 2
    d[0, P - 1] = 0.5
    t[:, T_DIFF:T_DIFF + P] = d
    t[:, T_TRI8:T_COLS] = np.tril(np.ones((NEXP, NEXP)), -1).reshape(-1)
    t[:, T_COLS:] = np.arange(T_WIDE)
    return t


def wait_for(eng, sem, n):
    if not isinstance(n, int) or n > 0:
        eng.wait_ge(sem, n)


class Chain:

    def __init__(self, eng, sem, base=0):
        self.eng, self.sem, self.base, self.n = eng, sem, base, 0

    def link(self, ins):
        self.n += 1
        ins.then_inc(self.sem, 1)
        self.eng.wait_ge(self.sem, self.base + self.n)


def build(nc, x, src, dst, wc, wn, bias, Wr, br, W1, b1, W2, b2, tab, out):
    f32, bf16, f16, i32 = mybir.dt.float32, mybir.dt.bfloat16, mybir.dt.float16, mybir.dt.int32
    f32r = mybir.dt.float32r
    ALU, ACT, AX = mybir.AluOpType, mybir.ActivationFunctionType, mybir.AxisListType.X

    beta_rows = nc.dram_tensor("beta_rows", (NS, H), f32, kind="Internal").ap()
    node_rows = nc.dram_tensor("node_rows", (NS, ROW), f32, kind="Internal").ap()

    ctx = ExitStack()
    with ctx:
        def sb(name, shape, dt):
            return ctx.enter_context(nc.sbuf_tensor(name, shape, dt))

        def pb(name, shape, dt=f32):
            return ctx.enter_context(nc.psum_tensor(name, shape, dt))

        def sem(name):
            return ctx.enter_context(nc.semaphore(name))

        OH = P + WC
        with nc.sbuf_tensor("beta", [P, 2, NT, H], f32r) as beta:
            with nc.sbuf_tensor("ring", [P, TPC, OH], bf16) as ring:
                with nc.sbuf_tensor("lists", [P, 4 * ETP], f32) as lists:
                    pass
        W1_LATE = -(-(2 * NT * H + 4 * ETP + TPC * OH // 2 - NEXP * KC * H) // (KC * H))
        W2_LATE = -(-2 * NT * H // (KC * H))
        w2_sb = sb("w2_sb", [P, NEXP * KC * H], f32)
        w1_sb = sb("w1_sb", [P, NEXP * KC * H], f32)
        with nc.sbuf_tensor("adj", [P, NT, NS], f16) as adj:
            with nc.sbuf_tensor("w_graph", [P, 2, KC, H], f32) as w_graph:
                pass
            with nc.sbuf_tensor("lhs", [P, 2, NT, P], f32r) as lhs:
                pass
        wn_sb, wc_sb = w_graph[:, 0, :, :], w_graph[:, 1, :, :]
        mid = sb("mid", [P, NT * NS // 2 + 2 * KC * H], f32)
        rows = mid[:, 0:TOKT * ROW].rearrange("p (j c) -> p j c", j=TOKT)
        wide_iota = mid[:, 0:T_WIDE]
        wide_hot = mid[:, T_WIDE:2 * T_WIDE]
        got_row = mid[:, 2 * T_WIDE:2 * T_WIDE + H]
        whole_beta = mid[:, 2 * T_WIDE + H:2 * T_WIDE + 2 * H]
        g0 = 2 * T_WIDE + 2 * H
        src_rel = mid[:, g0:g0 + ETP]
        gather_at = mid[:, g0 + ETP:g0 + 2 * ETP].bitcast(i32)
        xrow = sb("xrow", [P, NT * ROW], f32)
        X = xrow[:, :].rearrange("p (i c) -> p i c", i=NT)
        y_out = xrow[:, 0:H]
        b2_b = xrow[:, NT * ROW - NEXP * H:]
        assert NT * ROW >= (NEXP + 1) * H
        xT = sb("xT", [P, KC * P], f32)
        hid = sb("hid", [P, H], f32)[:, :]
        xn = sb("xn", [P, H], f32)
        bias_b = sb("bias_b", [P, H], f32)
        part = sb("part", [P, H], f32)
        hidT = part[:, :]
        chunk = sb("chunk", [P, SB, P], f16)
        lane_hot = chunk[:, :, :].bitcast(bf16)
        tabs = sb("tabs", [P, T_COLS], f32)
        ident = tabs[:, T_ID:T_ID + P]
        iota8 = tabs[:, T_IOTA:T_IOTA + NEXP]
        not_top = tabs[:, T_PLACE:T_PLACE + NT * NEXP].rearrange("p (i e) -> p i e", i=NT)
        tri8 = tabs[:, T_TRI8:T_COLS].rearrange("p (e f) -> p e f", e=NEXP)
        padding = tabs[:, T_PAD:T_PAD + NT]
        diff = sb("diff", [P, P], f16)
        trib = sb("trib", [P, P], bf16)
        onesb = sb("onesb", [P, P], bf16)
        onesf = sb("onesf", [P, P], f32)
        iota16 = sb("iota16", [P, WC], f16)
        r0 = W1_LATE * KC * H
        raw = w1_sb[:, r0:r0 + 2 * 3 * P].bitcast(i32).rearrange("p (a c) -> p a c", a=2)
        rawf = w1_sb[:, r0 + 6 * P:r0 + 12 * P].rearrange("p (a c) -> p a c", a=2)
        lane = w1_sb[:, r0 + 12 * P:r0 + 12 * P + ETP].bitcast(i32)
        block_i = w1_sb[:, r0 + 16 * P:r0 + 16 * P + ETP].bitcast(i32)
        missed = w1_sb[:, r0 + 20 * P:r0 + 20 * P + ETP]
        src_i = lists[:, 0:ETP].bitcast(i32)
        dst_f, lane_f, key = (lists[:, k * ETP:(k + 1) * ETP] for k in (1, 2, 3))
        lane_half = sb("lane_half", [P, ETP], f32)
        stats = sb("stats", [P, 6], f32)
        mv = sb("mv", [P, 2], f32)
        std = sb("std", [P, 1], f32)
        rstd = sb("rstd", [P, 1], f32)
        taker = sb("taker", [P, 3], f32)
        eps = sb("eps", [P, 1], f32)
        bank_sums = sb("bank_sums", [P, NT * QB], f32)
        checks = sb("checks", [P, 2], f32)
        flag_f = sb("flag_f", [P, 1], f32)
        flag_i = sb("flag_i", [P, 1], i32)
        count = sb("count", [P, 1], f32)
        rcount = sb("rcount", [P, 1], f32)
        stat2 = sb("stat2", [P, 6], f32)
        mv2 = sb("mv2", [P, 2], f32)
        std2 = sb("std2", [P, 1], f32)
        gather_col = sb("gather_col", [P, 1], i32)
        wr_sb = sb("wr_sb", [P, KC, NEXP], f32)
        br_b = sb("br_b", [P, NEXP], f32)
        b1_rows = sb("b1_rows", [NEXP * KC, P], f32)
        b1T = sb("b1T", [P, NEXP * KC], f32)
        used = [TOKT * ROW]

        def carve(n):
            used[0] += n
            assert used[0] <= NT * NS // 2 + 2 * KC * H
            return mid[:, used[0] - n:used[0]]
        logit, eqmax, shifted, expo, place = (carve(NT * NEXP).rearrange("p (i e) -> p i e", i=NT) for _ in range(5))
        hot = sb("hot", [P, NT, NEXP], bf16)
        top, best, esum, slot_f = (sb(n, [P, NT], f32) for n in ("top", "best", "esum", "slot_f"))
        tiles_i = sb("tiles_i", [P, NEXP], i32)
        before = sb("before", [P, NEXP, NEXP], f32)
        tiles_to = sb("tiles_to", [P, NEXP], f32)
        first_slot = sb("first_slot", [P, NEXP], f32)
        past = carve(TOKT * NEXP).rearrange("p (j e) -> p j e", j=TOKT)
        exp_f = sb("exp_f", [P, TOKT], f32)
        exp_i = sb("exp_i", [P, TOKT], i32)
        exp_hot = carve(TOKT * NEXP).rearrange("p (j e) -> p j e", j=TOKT)
        b1_sel = sb("b1_sel", [P, TOKT, KC], f32)
        b1_col = sb("b1_col", [P, KC], f32)
        row_at = sb("row_at", [P, 1], i32)
        gate = sb("gate", [P, NT], f32)
        gate_rest = sb("gate_rest", [P, NT], f32)
        pay = sb("pay", [P, NT, NPAY], bf16)
        slot_tile, slot_lane_f = sb("slot_tile", [P, NT], i32), sb("slot_lane_f", [P, NT], f32)
        tile_hot = carve(NT * TOKT).rearrange("p (i j) -> p i j", i=NT)
        sent = carve(NT * NPAY * TOKT // 2).bitcast(bf16).rearrange("p (i v j) -> p i v j", i=NT, v=NPAY)
        got = carve(3 * TOKT).rearrange("p (v j) -> p v j", v=3)
        out_f = sb("out_f", [P, TOKT], f32)
        node_i, out_i = sb("node_i", [P, TOKT], i32), sb("out_i", [P, TOKT], i32)
        gate_s = sb("gate_s", [P, TOKT], f32)

        bankA = [pb(f"bankA{q}", [P, H]) for q in range(QB)]
        bankT = pb("bankT", [P, H])
        bankB = pb("bankB", [P, H])
        bankC = pb("bankC", [P, H])
        bankR = pb("bankR", [P, H])

        names = """src_loaded dst_loaded tables_loaded small_loaded wc_loaded w1_loaded w2_loaded pad_rows_zero
            edge_pads_set iota_ready consts_ready edges_float edges_turned src_out dst_out stats_ready
            var_ready std_ready rstd_ready xn_ready bias_added xT_turned xT_ready beta_done beta_hi
            beta_rest lhs_ready alpha_done alpha_added hot_ready tiles_done bank_out turned turned_out
            sums_checked checks_summed flag_ready dve_pre took took_slow counts_done sums_done x1_ready
            x1_kept dve_fast dve_slow var2_ready std2_ready xn2_ready xn2_turned xT2_ready logits_done
            shift_ready exp_ready chosen ranked dve_route slots_ready lanes_ready experts_ready b1_ready
            b1_turned b2_loaded b2_added stairs_ready rows_kept rows_stored later_rows sent_ready at_slots
            nodes_ready xs_ready xs_turned xs_out h_done h_out h_turned hT_ready y_done y_ready y_stored
            beta_whole beta_stored wide_loaded slow_lists col_ready got_rows wide_ready edge_summed slow_x1
            b1col_ready""".split()
        S = {n: sem(n) for n in names}
        x_loaded = [sem(f"x_loaded{i}") for i in range(NT)]
        wn_loaded = [sem(f"wn_loaded{c}") for c in range(KC)]
        rows_got = [sem(f"rows_got{j}") for j in range(AHEAD)]

        def s(name):
            return S[name]

        w1v = w1_sb[:, :].rearrange("p (e k n) -> p e k n", e=NEXP, k=KC)
        w2v = w2_sb[:, :].rearrange("p (e k n) -> p e k n", e=NEXP, k=KC)

        block = ctx.enter_context(nc.Block())

        @block.sync
        def _(sp):
            sp.dma_start(X[:, 0, 0:H], x[0:P, :]).then_inc(x_loaded[0], 16)
            sp.wait_ge(s("edge_pads_set"), 1)
            for a, (ids, loaded) in enumerate(((src, "src_loaded"), (dst, "dst_loaded"))):
                for c in range(2):
                    sp.dma_start(raw[:, a, c * P:(c + 1) * P],
                                 ids[c * P * P:(c + 1) * P * P].rearrange("(t e) -> t e", e=P)).then_inc(s(loaded), 16)
                full = (E_EDGES - 2 * P * P) // P
                at = (2 * P + full) * P
                sp.dma_start(raw[0:full, a, 2 * P:3 * P],
                             ids[2 * P * P:at].rearrange("(t e) -> t e", e=P)).then_inc(s(loaded), 16)
                sp.dma_start(raw[full:full + 1, a, 2 * P:2 * P + E_EDGES - at],
                             ids[at:E_EDGES].rearrange("(t e) -> t e", t=1)).then_inc(s(loaded), 16)
            for c in range(KC):
                sp.dma_start(wn_sb[:, c, :], wn[c * P:(c + 1) * P, :]).then_inc(wn_loaded[c], 16)
            sp.dma_start(X[:, 1, 0:H], x[P:2 * P, :]).then_inc(x_loaded[1], 16)
            sp.dma_start(wc_sb, wc.rearrange("(k p) n -> p k n", p=P)).then_inc(s("wc_loaded"), 16)
            for i in range(2, NT):
                n = P if i < NT - 1 else LAST
                if i == NT - 1:
                    sp.wait_ge(s("pad_rows_zero"), 1)
                sp.dma_start(X[0:n, i, 0:H], x[i * P:i * P + n, :]).then_inc(x_loaded[i], 16)
            sp.wait_ge(s("iota_ready"), 3)
            for e in range(W1_LATE, NEXP):
                sp.dma_start(w1v[:, e], W1[e].rearrange("(k p) n -> p k n", p=P)).then_inc(s("w1_loaded"), 16)
            sp.wait_ge(s("tiles_done"), NT * NG)

            def after_ring():
                for e in range(W1_LATE):
                    sp.dma_start(w1v[:, e], W1[e].rearrange("(k p) n -> p k n", p=P)).then_inc(s("w1_loaded"), 16)
                for e in range(W2_LATE, NEXP):
                    sp.dma_start(w2v[:, e], W2[e].rearrange("(k p) n -> p k n", p=P)).then_inc(s("w2_loaded"), 16)
            sp.wait_ge(s("flag_ready"), 1)
            slow = sp.value_load(flag_i[0:1, 0:1], min_val=0, max_val=1 << 30)

            def store_rows():
                with sp.Fori(0, NT) as i:
                    sp.wait_ge(s("x1_kept"), i + 1)
                    sp.wait_ge(s("rows_kept"), i + 1)
                    sp.dma_start(node_rows[bass.ds(i * P, P), :],
                                 X[:, bass.ds(i, 1), :].squeeze(1)).then_inc(s("rows_stored"), 16)
            with sp.If(slow == 0):
                after_ring()
                store_rows()
            with sp.Else():
                sp.wait_ge(s("lhs_ready"), 3)
                sp.dma_start(wide_iota, tab[:, T_COLS:]).then_inc(s("wide_loaded"), 16)

                def store_beta(i):
                    sp.wait_ge(s("beta_whole"), i + 1)
                    sp.dma_start(beta_rows[bass.ds(i * P, P), :], whole_beta).then_inc(s("beta_stored"), 16)
                with sp.Fori(0, NT) as i:
                    store_beta(i)
                sp.wait_ge(s("slow_x1"), NT)
                after_ring()
                store_rows()
            for e in range(W2_LATE):
                if e == W2_LATE - 1:
                    sp.wait_ge(rows_got[AHEAD - 1], 16)
                sp.dma_start(w2v[:, e], W2[e].rearrange("(k p) n -> p k n", p=P)).then_inc(s("w2_loaded"), 16)
            sp.wait_ge(s("rows_stored"), 16 * NT)
            sp.dma_start(b2_b, b2.rearrange("e n -> (e n)").partition_broadcast(P)).then_inc(s("b2_loaded"), 16)
            sp.wait_ge(s("y_stored"), 16 * TOKT)

        @block.gpsimd
        def _(pool):
            pool.dma_start(tabs[:, :], tab[:, 0:T_COLS]).then_inc(s("tables_loaded"), 16)
            pool.memset(raw[:, 0, 2 * P:3 * P], PAD_SRC)
            pool.memset(raw[:, 1, 2 * P:3 * P], PAD_DST).then_inc(s("edge_pads_set"), 1)
            pool.memset(onesb[:, :], 1.0)
            pool.memset(onesf[:, :], 1.0)
            pool.memset(eps[:, :], EPS).then_inc(s("consts_ready"), 1)
            pool.dma_start(bias_b[:, :], bias.partition_broadcast(P)).then_inc(s("small_loaded"), 16)
            pool.dma_start(br_b[:, :], br.partition_broadcast(P)).then_inc(s("small_loaded"), 16)
            pool.dma_start(wr_sb[:, :, :], Wr.rearrange("(k p) n -> p k n", p=P)).then_inc(s("small_loaded"), 16)
            pool.dma_start(b1_rows[:, :], b1.rearrange("e (c p) -> (e c) p", p=P)).then_inc(s("small_loaded"), 16)
            def take_wait(took, col):
                pool.tensor_tensor(taker[:, col:col + 1], eps[:, :], eps[:, :], ALU.add).then_inc(took, 1)
            last_node, last_beta = pool.to_reg(N - 1), pool.to_reg(NS - 1)
            pool.wait_ge(s("small_loaded"), 64)
            with pool.Fori(0, NT) as i:
                pool.wait_ge(s("xn_ready"), i + 1)
                pool.tensor_tensor(X[:, bass.ds(i, 1), 0:H].squeeze(1), X[:, bass.ds(i, 1), 0:H].squeeze(1),
                                   bias_b[:, :], ALU.add).then_inc(s("bias_added"), 1)
            pool.wait_ge(s("flag_ready"), 1)
            slow = pool.value_load(flag_i[0:1, 0:1], min_val=0, max_val=1 << 30)
            with pool.If(slow == 0):
                pool.nop()
            with pool.Else():
                pool.wait_ge(s("beta_stored"), 16 * NT)
                pool.wait_ge(s("slow_lists"), 2)
                def gather(t, h):
                    wait_for(pool, s("edge_summed"), t + h * ETP)
                    pool.tensor_copy(gather_col[:, :], gather_at[:, bass.ds(t, 1)]).then_inc(s("col_ready"), 1)
                    wait_for(pool, s("took_slow"), t + h * ETP)
                    pool.wait_ge(s("col_ready"), t + (h * ETP + 1))
                    take_wait(s("took_slow"), 2)
                    pool.indirect_dma_start(got_row, None, beta_rows,
                                            bass.IndirectOffsetOnAxis(ap=gather_col[:, :], axis=0),
                                            bounds_check=last_beta, oob_is_err=False).then_inc(s("got_rows"), 16)
                for h in range(2):
                    gather(0, h)
                    with pool.Fori(1, ETP) as t:
                        gather(t, h)
            pool.nop()
            pool.wait_ge(s("slots_ready"), 1)
            for i in range(POOL_HOTS):
                last = pool.tensor_scalar(lane_hot[:, i, :], iota16[:, 0:P], slot_lane_f[:, i:i + 1], None, ALU.is_equal)
            last.then_inc(s("lanes_ready"), 1)
            pool.wait_ge(s("rows_stored"), 16 * NT)
            pool.wait_ge(s("nodes_ready"), 1)
            for j in range(TOKT):
                pool.indirect_dma_start(rows[:, j, :], None, node_rows,
                                        bass.IndirectOffsetOnAxis(ap=node_i[:, j:j + 1], axis=0),
                                        bounds_check=last_beta, oob_is_err=False
                                        ).then_inc(rows_got[j] if j < AHEAD else s("later_rows"), 16)
            def store_result(j):
                wait_for(pool, s("took"), j)
                pool.wait_ge(s("y_ready"), j + 1)
                take_wait(s("took"), 1)
                pool.indirect_dma_start(out, bass.IndirectOffsetOnAxis(ap=row_at[:, :], axis=0), y_out, None,
                                        bounds_check=last_node, oob_is_err=False).then_inc(s("y_stored"), 16)
            store_result(0)
            with pool.Fori(1, TOKT) as j:
                store_result(j)

        @block.scalar
        def _(act):
            def bank_evac(c, q):
                nc.scalar.activation(chunk[:, :, q * QN:(q + 1) * QN],
                                     bankA[q][:, 0:QC].rearrange("p (d s) -> p s d", s=SB), ACT.Copy,
                                     accum_out=bank_sums[:, bass.ds(c * QB + q, 1)]).then_inc(s("bank_out"), 1)

            def turned_evac(c, k):
                n = min(TURN, SB - k * TURN) * P
                act.wait_ge(s("turned"), c * ROUNDS + (k + 1))
                nc.scalar.copy(adj[:, bass.ds(c, 1), k * TURN * P:k * TURN * P + n].squeeze(1),
                               bankR[:, 0:n]).then_inc(s("turned_out"), 1)

            def widen(i, par, d0=0, d1=NT):
                nc.scalar.copy(lhs[:, par, d0:d1, :], adj[:, d0:d1, bass.ds(i * P, P)]).then_inc(s("lhs_ready"), 1)

            def stairs(i, g, first):
                if not first:
                    act.wait_ge(s("tiles_done"), i * NG + (g + 1 - NG))
                for r in range(g * GRP, (g + 1) * GRP):
                    if r in (ACT_TILES_0 if first else ACT_TILES):
                        last = nc.scalar.activation(ring[:, r, 0:P], iota16[:, 0:P], ACT.Sign, scale=-1.0,
                                                    bias=lane_half[:, bass.ds(i * TPC + r, 1)])
                last.then_inc(s("stairs_ready"), 1)

            def root(i):
                act.wait_ge(s("var_ready"), i + 1)
                nc.scalar.activation(std[:, :], mv[:, 1:2], ACT.Sqrt, bias=eps[:, 0:1]).then_inc(s("std_ready"), 1)

            def xT_copy(i):
                act.wait_ge(s("xT_turned"), i + 1)
                nc.scalar.copy(xT[:, :], bankT[:, :]).then_inc(s("xT_ready"), 1)

            act.wait_ge(s("consts_ready"), 1)
            root(0)

            def body(i, first=False, final=False):
                def bank(q):
                    act.wait_ge(s("tiles_done"), i * NG + (CLOSE[(0, q)] // GRP + 1))
                    bank_evac(i, q)
                if first:
                    xT_copy(0)
                    act.wait_ge(s("edges_turned"), 2)
                    nc.scalar.copy(dst_f, bankA[1][:, 0:ETP]).then_inc(s("dst_out"), 1)
                    act.wait_ge(s("iota_ready"), 2)
                    for g in range(4):
                        stairs(i, g, first)
                    root(1)
                else:
                    if not final:
                        root(i + 1)
                    act.wait_ge(s("alpha_done"), i)
                    xT_copy(i)
                    act.wait_ge(s("tiles_done"), i * NG + (CLOSE[(-1, QB - 1)] // GRP + 1))
                    bank_evac(i - 1, QB - 1)
                    for g in range(2, 5):
                        stairs(i, g, first)
                    turned_evac(i - 1, 0)
                    stairs(i, 5, first)
                act.wait_ge(s("beta_done"), i + 1)
                nc.scalar.copy(beta[:, 0, bass.ds(i, 1), :].squeeze(1), bankB[:, :]).then_inc(s("beta_hi"), 1)
                if first:
                    stairs(i, 4, first)
                    stairs(i, 5, first)
                stairs(i, 6, first)
                if not first:
                    turned_evac(i - 1, 1)
                stairs(i, 7, first)
                stairs(i, 8, first)
                stairs(i, 9, first)
                stairs(i, 10, first)
                if not first:
                    turned_evac(i - 1, 2)
                if final:
                    act.wait_ge(s("alpha_done"), NT)
                    act.wait_ge(s("turned_out"), ROUNDS * (NT - 1))
                    widen(0, 0, 0, NT - 1)
                bank(0)
                bank(1)
                if not final:
                    stairs(i + 1, 0, False)
                    stairs(i + 1, 1, False)
                bank(2)

            body(0, True)
            with act.Fori(1, NT - 1) as i:
                body(i)
            body(NT - 1, final=True)
            act.wait_ge(s("tiles_done"), NT * NG)
            bank_evac(NT - 1, QB - 1)
            turned_evac(NT - 1, 0)
            act.wait_ge(s("turned_out"), ROUNDS * (NT - 1) + 1)
            widen(0, 0, NT - 1, NT)
            turned_evac(NT - 1, 1)
            turned_evac(NT - 1, 2)
            widen(1, 1)

            def second_norm(i):
                act.wait_ge(s("var2_ready"), i + 1)
                nc.scalar.activation(std2[:, :], mv2[:, 1:2], ACT.Sqrt, bias=eps[:, 0:1]).then_inc(s("std2_ready"), 1)
                nc.scalar.copy(X[:, bass.ds(i, 1), 0:H].squeeze(1), part[:, :]).then_inc(s("x1_kept"), 1)
                act.wait_ge(s("xn2_turned"), i + 1)
                wait_for(act, s("logits_done"), i)
                nc.scalar.copy(xT[:, :], bankT[:, :]).then_inc(s("xT2_ready"), 1)

            act.wait_ge(s("flag_ready"), 1)
            slow = act.value_load(flag_i[0:1, 0:1], min_val=0, max_val=1 << 30)
            with act.If(slow == 0):
                def block_out(i, par, final=False):
                    if not final:
                        act.wait_ge(s("sums_done"), i + 1)
                        widen(i + 2, par)
                    second_norm(i)
                block_out(0, 0)
                block_out(1, 1)
                with act.Fori(1, NT // 2 - 1) as m:
                    for par in range(2):
                        block_out(m * 2 + par, par)
                block_out(NT - 2, 0, final=True)
                block_out(NT - 1, 1, final=True)
            with act.Else():
                second_norm(0)
                with act.Fori(1, NT) as i:
                    second_norm(i)
            act.nop()

            act.wait_ge(s("shift_ready"), 1)
            nc.scalar.activation(expo[:, :, :], shifted[:, :, :], ACT.Exp).then_inc(s("exp_ready"), 1)

            def xs_evac(j):
                act.wait_ge(s("xs_turned"), j + 1)
                nc.scalar.copy(xT[:, :], bankT[:, :]).then_inc(s("xs_out"), 1)

            def relu(j):
                act.wait_ge(s("h_turned"), j + 1)
                act.wait_ge(s("b1col_ready"), j + 1)
                for c in range(KC):
                    last = nc.scalar.activation(hidT[:, c * P:(c + 1) * P], bankC[:, c * P:(c + 1) * P], ACT.Relu,
                                                bias=b1_col[:, c:c + 1])
                last.then_inc(s("hT_ready"), 1)

            xs_evac(0)
            with act.Fori(0, TOKT - 1) as j:
                xs_evac(j + 1)
                relu(j)
            relu(TOKT - 1)

        @block.vector
        def _(dve):
            V = nc.vector
            ch = Chain(dve, s("dve_pre"))
            V.memset(X[96:P, NT - 1, 0:H], 0.0).then_inc(s("pad_rows_zero"), 1)
            dve.wait_ge(x_loaded[0], 16)
            V.bn_stats(stats[:, :], X[:, 0, 0:H]).then_inc(s("stats_ready"), 1)
            dve.wait_ge(s("stats_ready"), 1)
            V.bn_aggr(mv[:, :], stats[:, :]).then_inc(s("var_ready"), 1)
            dve.wait_ge(s("tables_loaded"), 16)
            V.tensor_copy(iota16[:, :], tabs[:, T_IOTA:T_IOTA + WC])
            V.tensor_copy(trib[:, :], tabs[:, T_TRI:T_TRI + P])
            V.tensor_copy(pay[:, :, :], tabs[:, T_PAY:T_PAY + NT * NPAY].rearrange("p (i v) -> p i v", i=NT))
            V.tensor_copy(diff[:, :], tabs[:, T_DIFF:T_DIFF + P]).then_inc(s("iota_ready"), 1)
            dve.wait_ge(s("std_ready"), 1)
            V.reciprocal(rstd[:, :], std[:, :]).then_inc(s("rstd_ready"), 1)
            dve.wait_ge(s("rstd_ready"), 1)
            V.tensor_scalar(xn[:, :], X[:, 0, 0:H], mv[:, 0:1], rstd[:, :], ALU.subtract,
                            ALU.mult).then_inc(s("xn_ready"), 1)
            for a, loaded in enumerate(("src_loaded", "dst_loaded")):
                dve.wait_ge(s(loaded), 16 * 4)
                V.tensor_copy(rawf[:, a, :], raw[:, a, :]).then_inc(s("edges_float"), 1)
            dve.wait_ge(s("edges_turned"), 1)
            V.tensor_copy(src_i, bankA[0][:, 0:ETP]).then_inc(s("src_out"), 1)
            dve.wait_ge(s("src_out"), 1)
            V.tensor_scalar(lane, src_i, P - 1, None, ALU.bitwise_and)
            ch.link(V.tensor_scalar(block_i, src_i, 7, None, ALU.arith_shift_right))
            V.tensor_copy(lane_f, lane)
            V.tensor_scalar(lane_half[:, :], lane, 0.5, None, ALU.add)
            dve.wait_ge(s("dst_out"), 1)
            ch.link(V.scalar_tensor_tensor(key, dst_f, float(SB), block_i, ALU.mult, ALU.add))
            V.tensor_tensor(key, key, tabs[:, T_BASE:T_BASE + ETP], ALU.subtract).then_inc(s("iota_ready"), 1)
            dve.wait_ge(s("iota_ready"), 2)

            def add_alpha(i):
                dve.wait_ge(s("alpha_done"), i + 1)
                dve.wait_ge(s("bias_added"), i + 1)
                V.tensor_tensor(X[:, bass.ds(i, 1), 0:H].squeeze(1), X[:, bass.ds(i, 1), 0:H].squeeze(1),
                                bankC[:, :], ALU.add).then_inc(s("alpha_added"), 1)

            def body(i, first=False, second=False, final=False):
                on_act = ACT_TILES_0 if first else ACT_TILES
                for g in range(NG):
                    if not first:
                        dve.wait_ge(s("tiles_done"), i * NG + (g + 1 - NG))
                    if g == 1 and not final:
                        dve.wait_ge(s("stats_ready"), i + 2)
                        dve.wait_ge(s("xn_ready"), i + 1)
                    for r in range(g * GRP, (g + 1) * GRP):
                        if r not in on_act:
                            V.tensor_scalar(ring[:, r, 0:P], iota16[:, 0:P], lane_f[:, bass.ds(i * TPC + r, 1)], 0.5,
                                            ALU.is_le, ALU.subtract)
                        last = V.tensor_scalar(ring[:, r, P:OH], iota16[:, :], key[:, bass.ds(i * TPC + r, 1)],
                                               1.0 if r in on_act else 2.0, ALU.is_equal, ALU.mult)
                    last.then_inc(s("hot_ready"), 1)
                    if g == 0:
                        if first:
                            dve.wait_ge(x_loaded[1], 16)
                        if not final:
                            V.bn_stats(stats[:, :], X[:, bass.ds(i + 1, 1), 0:H].squeeze(1)).then_inc(s("stats_ready"), 1)
                    if g == 1 and not final:
                        V.bn_aggr(mv[:, :], stats[:, :]).then_inc(s("var_ready"), 1)
                    if g == 2 and not first:
                        add_alpha(i - 1)
                    if g == 3 and not final:
                        dve.wait_ge(s("std_ready"), i + 2)
                        V.reciprocal(rstd[:, :], std[:, :]).then_inc(s("rstd_ready"), 1)
                    if g == 4 and not final:
                        dve.wait_ge(s("rstd_ready"), i + 2)
                        dve.wait_ge(s("xT_turned"), i + 1)
                        V.tensor_scalar(xn[:, :], X[:, bass.ds(i + 1, 1), 0:H].squeeze(1), mv[:, 0:1], rstd[:, :],
                                        ALU.subtract, ALU.mult).then_inc(s("xn_ready"), 1)
                    if g == 7 and second:
                        ch.link(V.tensor_scalar(missed, key, float(WC), None, ALU.is_ge))
                        ch.link(V.scalar_tensor_tensor(missed, key, 0.0, missed, ALU.is_lt, ALU.add))
                        V.tensor_reduce(checks[:, 0:1], missed, AX, ALU.add).then_inc(s("iota_ready"), 1)
                    if g == 9:
                        dve.wait_ge(s("beta_hi"), i + 1)
                        V.tensor_tensor(beta[:, 1, bass.ds(i, 1), :].squeeze(1), bankB[:, :],
                                        beta[:, 0, bass.ds(i, 1), :].squeeze(1), ALU.subtract).then_inc(s("beta_rest"), 1)

            body(0, first=True)
            dve.wait_ge(x_loaded[2], 16)
            body(1, second=True)
            for i in range(3, NT):
                dve.wait_ge(x_loaded[i], 16)
            with dve.Fori(2, NT - 1) as i:
                body(i)
            body(NT - 1, final=True)
            add_alpha(NT - 1)

            dve.wait_ge(s("bank_out"), NT * QB)
            ch.link(V.tensor_reduce(count[:, :], bank_sums[:, :], AX, ALU.max))
            V.tensor_scalar(checks[:, 1:2], count[:, :], float(ADJ_EXACT), None, ALU.is_ge).then_inc(s("sums_checked"), 1)
            dve.wait_ge(s("checks_summed"), 1)
            ch.link(V.tensor_reduce(flag_f[:, :], bankB[:, 0:2], AX, ALU.add))
            V.tensor_scalar(flag_i[:, :], flag_f[:, :], float(N_PAD_EDGES), None, ALU.subtract).then_inc(s("flag_ready"), 1)
            dve.wait_ge(s("b1_turned"), 1)
            V.tensor_copy(b1T[:, :], bankC[:, 0:NEXP * KC]).then_inc(s("b1_ready"), 1)

            def second_norm(i, ch):
                ch.link(V.bn_stats(stat2[:, :], part[:, :]))
                V.tensor_copy(taker[:, 0:1], stat2[:, 0:1])
                V.bn_aggr(mv2[:, 0:2], stat2[:, :]).then_inc(s("var2_ready"), 1)
                dve.wait_ge(s("std2_ready"), i + 1)
                ch.link(V.reciprocal(mv2[:, 1:2], std2[:, :]))
                wait_for(dve, s("xn2_turned"), i)
                V.tensor_scalar(xn[:, :], part[:, :], mv2[:, 0:1], mv2[:, 1:2], ALU.subtract, ALU.mult).then_inc(s("xn2_ready"), 1)
                V.tensor_copy(X[:, bass.ds(i, 1), H:H + 2].squeeze(1), mv2[:, :]).then_inc(s("rows_kept"), 1)

            dve.wait_ge(s("flag_ready"), 1)
            slow = dve.value_load(flag_i[0:1, 0:1], min_val=0, max_val=1 << 30)
            with dve.If(slow == 0):
                def graph_out(i, par):
                    c = Chain(dve, s("dve_fast"), i * 4)
                    Xi = X[:, bass.ds(i, 1), 0:H].squeeze(1)
                    dve.wait_ge(s("counts_done"), i + 1)
                    c.link(V.tensor_tensor(count[:, :], bankA[2 + par][:, 0:1], padding[:, bass.ds(i, 1)], ALU.add))
                    c.link(V.reciprocal(rcount[:, :], count[:, :]))
                    dve.wait_ge(s("sums_done"), i + 1)
                    wait_for(dve, s("x1_kept"), i)
                    V.scalar_tensor_tensor(part[:, :], bankA[par][:, :], rcount[:, 0:1], Xi, ALU.mult, ALU.add).then_inc(s("x1_ready"), 1)
                    dve.wait_ge(s("x1_ready"), i + 1)
                    second_norm(i, c)
                    assert c.n == 4
                graph_out(0, 0)
                graph_out(1, 1)
                with dve.Fori(1, NT // 2) as m:
                    for par in range(2):
                        graph_out(m * 2 + par, par)
            with dve.Else():
                dve.wait_ge(s("lhs_ready"), 3)
                def rejoin(i):
                    wait_for(dve, s("beta_stored"), i * 16)
                    V.tensor_tensor(whole_beta, beta[:, 0, bass.ds(i, 1), :].squeeze(1),
                                    beta[:, 1, bass.ds(i, 1), :].squeeze(1), ALU.add).then_inc(s("beta_whole"), 1)
                rejoin(0)
                with dve.Fori(1, NT) as i:
                    rejoin(i)
                V.tensor_scalar(gather_at, dst_f, float(NS - 1), None, ALU.min).then_inc(s("slow_lists"), 1)
                dve.wait_ge(s("wide_loaded"), 16)
                for h in range(2):
                    V.tensor_scalar(src_rel, src_i, float(h * T_WIDE), None, ALU.subtract).then_inc(s("slow_lists"), 1)
                    dve.wait_ge(s("slow_lists"), 2 + h)
                    def wide(t):
                        wait_for(dve, s("edge_summed"), t + h * ETP)
                        V.tensor_scalar(wide_hot, wide_iota, src_rel[:, bass.ds(t, 1)], None,
                                        ALU.is_equal).then_inc(s("wide_ready"), 1)
                    wide(0)
                    with dve.Fori(1, ETP) as t:
                        wide(t)
                    dve.wait_ge(s("edge_summed"), (h + 1) * ETP)
                    c = Chain(dve, s("dve_slow"), 2 * HB * h)
                    sums = [bankA[0], bankA[1], bankA[2], bankA[3], bankT]
                    for b in range(HB):
                        i = h * HB + b
                        c.link(V.tensor_tensor(count[:, :], bankB[:, b:b + 1], padding[:, i:i + 1], ALU.add))
                        c.link(V.reciprocal(rcount[:, :], count[:, :]))
                        V.scalar_tensor_tensor(X[:, i, 0:H], sums[b][:, :], rcount[:, 0:1], X[:, i, 0:H],
                                               ALU.mult, ALU.add).then_inc(s("slow_x1"), 1)
                dve.wait_ge(s("slow_x1"), NT)
                def block_norm(i):
                    wait_for(dve, s("x1_kept"), i)
                    wait_for(dve, s("xn2_ready"), i)
                    V.tensor_copy(part[:, :], X[:, bass.ds(i, 1), 0:H].squeeze(1)).then_inc(s("x1_ready"), 1)
                    dve.wait_ge(s("x1_ready"), i + 1)
                    second_norm(i, Chain(dve, s("dve_slow"), 4 * HB + i * 2))
                block_norm(0)
                with dve.Fori(1, NT) as i:
                    block_norm(i)
            dve.nop()

            ch = Chain(dve, s("dve_route"))
            dve.wait_ge(s("logits_done"), NT)
            full = [P, NT, NEXP]

            def over_exp(ap):
                return ap.unsqueeze(2).broadcast_to(full)

            def over_tiles(ap):
                return ap.unsqueeze(1).broadcast_to(full)
            logits = bankB[:, 0:NT * NEXP].rearrange("p (i e) -> p i e", e=NEXP)
            ch.link(V.tensor_tensor(logit[:, :, :], logits, over_tiles(br_b[:, :]), ALU.add))
            ch.link(V.tensor_reduce(top[:, :], logit[:, :, :], AX, ALU.max))
            V.tensor_tensor(shifted[:, :, :], logit[:, :, :], over_exp(top[:, :]), ALU.subtract).then_inc(s("shift_ready"), 1)
            ch.link(V.tensor_tensor(eqmax[:, :, :], logit[:, :, :], over_exp(top[:, :]), ALU.is_equal))
            ch.link(V.scalar_tensor_tensor(place[:, :, :], eqmax[:, :, :], -float(NEXP - 1), not_top, ALU.mult, ALU.add))
            ch.link(V.tensor_reduce(best[:, :], place[:, :, :], AX, ALU.min))
            V.tensor_tensor(hot[:, :, :], over_tiles(iota8), over_exp(best[:, :]), ALU.is_equal).then_inc(s("chosen"), 1)
            dve.wait_ge(s("exp_ready"), 1)
            ch.link(V.tensor_reduce(esum[:, :], expo[:, :, :], AX, ALU.add))
            ch.link(V.reciprocal(gate[:, :], esum[:, :]))
            ch.link(V.tensor_tensor(gate[:, :], gate[:, :], pay[:, :, 2], ALU.mult))
            dve.wait_ge(s("ranked"), 1)
            ch.link(V.tensor_scalar(tiles_i[:, :], bankC[:, P:P + NEXP], P / 2 - 0.5, 1.0 / P, ALU.add, ALU.mult))
            ch.link(V.tensor_tensor(before[:, :, :], tri8, tiles_i[:, :].unsqueeze(1).broadcast_to([P, NEXP, NEXP]), ALU.mult))
            ch.link(V.tensor_reduce(first_slot[:, :], before[:, :, :], AX, ALU.add))
            ch.link(V.scalar_tensor_tensor(place[:, :, :], over_tiles(first_slot[:, :]), float(P),
                                           bankC[:, 0:NT * NEXP].rearrange("p (i e) -> p i e", e=NEXP), ALU.mult, ALU.add))
            ch.link(V.tensor_tensor(place[:, :, :], place[:, :, :], hot[:, :, :], ALU.mult))
            ch.link(V.tensor_reduce(slot_f[:, :], place[:, :, :], AX, ALU.add))
            ch.link(V.tensor_scalar(slot_tile[:, :], slot_f[:, :], P / 2 - 0.5, 1.0 / P, ALU.subtract, ALU.mult))
            V.scalar_tensor_tensor(slot_lane_f[:, :], slot_tile[:, :], -float(P), slot_f[:, :], ALU.mult,
                                   ALU.add).then_inc(s("slots_ready"), 1)
            dve.wait_ge(s("slots_ready"), 1)
            sh = [P, NT, TOKT]
            V.tensor_tensor(tile_hot[:, :, :], tabs[:, T_IOTA:T_IOTA + TOKT].unsqueeze(1).broadcast_to(sh),
                            slot_tile[:, :].unsqueeze(2).broadcast_to(sh), ALU.is_equal)
            for i in range(POOL_HOTS, NT):
                last = V.tensor_scalar(lane_hot[:, i, :], iota16[:, 0:P], slot_lane_f[:, i:i + 1], None, ALU.is_equal)
            ch.link(last)
            def send(v):
                sh = [P, NT, NPAY // 2, TOKT]
                V.tensor_tensor(sent[:, :, v:v + NPAY // 2, :], tile_hot[:, :, :].unsqueeze(2).broadcast_to(sh),
                                pay[:, :, v:v + NPAY // 2].unsqueeze(3).broadcast_to(sh), ALU.mult).then_inc(s("sent_ready"), 1)
            send(0)
            dve.wait_ge(s("at_slots"), 1)
            V.tensor_copy(node_i[:, :], bankC[:, 2 * P:2 * P + TOKT]).then_inc(s("nodes_ready"), 1)
            dve.wait_ge(s("nodes_ready"), 1)
            ch.link(V.scalar_tensor_tensor(out_f[:, :], bankC[:, 2 * P + TOKT:2 * P + 2 * TOKT], -float(SLOTS),
                                           node_i[:, :], ALU.mult, ALU.add))
            V.tensor_scalar(out_i[:, :], out_f[:, :], float(SLOTS), None, ALU.add)
            ft = [P, TOKT, NEXP]
            ch.link(V.tensor_tensor(tiles_to[:, :], first_slot[:, :], tiles_i[:, :], ALU.add))
            ch.link(V.tensor_tensor(past[:, :, :], tabs[:, T_IOTA:T_IOTA + TOKT].unsqueeze(2).broadcast_to(ft),
                                    tiles_to[:, :].unsqueeze(1).broadcast_to(ft), ALU.is_ge))
            ch.link(V.tensor_reduce(exp_f[:, :], past[:, :, :], AX, ALU.add))
            ch.link(V.tensor_scalar(exp_f[:, :], exp_f[:, :], float(NEXP - 1), None, ALU.min))
            V.tensor_copy(exp_i[:, :], exp_f[:, :]).then_inc(s("experts_ready"), 1)
            ch.link(V.tensor_tensor(exp_hot[:, :, :], iota8.unsqueeze(1).broadcast_to(ft),
                                    exp_f[:, :].unsqueeze(2).broadcast_to(ft), ALU.is_equal))
            dve.wait_ge(s("b1_ready"), 1)
            b1v = b1T[:, :].rearrange("p (e c) -> p c e", c=KC)
            assert TOKT * NEXP <= H
            for c in range(KC):
                prod = (bias_b, part)[c % 2][:, 0:TOKT * NEXP].rearrange("p (j e) -> p j e", e=NEXP)
                ch.link(V.tensor_tensor(prod, exp_hot[:, :, :], b1v[:, c:c + 1, :].broadcast_to(ft), ALU.mult))
                last = V.tensor_reduce(b1_sel[:, :, c:c + 1].squeeze(2), prod, AX, ALU.add)
            ch.link(last)

            def xs_norm(j):
                wait_for(dve, s("xs_turned"), j)
                r = rows[:, bass.ds(j, 1), :].squeeze(1)
                V.tensor_scalar(xn[:, :], r[:, 0:H], r[:, H:H + 1], r[:, H + 1:H + 2], ALU.subtract,
                                ALU.mult).then_inc(s("xs_ready"), 1)

            def h_evac(j):
                dve.wait_ge(s("h_done"), j + 1)
                V.tensor_copy(hid, bankB[:, :]).then_inc(s("h_out"), 1)
                wait_for(dve, s("hT_ready"), j)
                V.tensor_copy(b1_col[:, :], b1_sel[:, bass.ds(j, 1), :].squeeze(1)).then_inc(s("b1col_ready"), 1)

            def add_b2(j):
                e = dve.value_load(exp_i[0:1, bass.ds(j, 1)], min_val=0, max_val=NEXP - 1)
                r = rows[:, bass.ds(j, 1), 0:H].squeeze(1)
                V.scalar_tensor_tensor(r, b2_b[:, bass.ds(e * H, H)], gate_s[:, bass.ds(j, 1)], r, ALU.mult,
                                       ALU.add).then_inc(s("b2_added"), 1)

            def result(j):
                dve.wait_ge(s("b2_added"), j + 1)
                dve.wait_ge(s("y_done"), j + 1)
                wait_for(dve, s("y_stored"), j * 16)
                r = rows[:, bass.ds(j, 1), :].squeeze(1)
                V.tensor_copy(row_at[:, :], out_i[:, bass.ds(j, 1)])
                V.scalar_tensor_tensor(y_out, bankA[0][:, :], gate_s[:, bass.ds(j, 1)], r[:, 0:H], ALU.mult,
                                       ALU.add).then_inc(s("y_ready"), 1)

            dve.wait_ge(rows_got[0], 16)
            xs_norm(0)
            ch.link(V.tensor_copy(pay[:, :, 3], gate[:, :]))
            ch.link(V.tensor_tensor(gate_rest[:, :], gate[:, :], pay[:, :, 3], ALU.subtract))
            ch.link(V.tensor_copy(pay[:, :, 4], gate_rest[:, :]))
            ch.link(V.tensor_tensor(pay[:, :, 5], gate_rest[:, :], pay[:, :, 4], ALU.subtract))
            send(NPAY // 2)
            dve.wait_ge(rows_got[1], 16)
            xs_norm(1)
            h_evac(0)
            dve.wait_ge(s("at_slots"), 2)
            ch.link(V.tensor_copy(got[:, :, :], bankR[:, 0:3 * TOKT].rearrange("p (v j) -> p v j", v=3)))
            ch.link(V.tensor_tensor(gate_s[:, :], got[:, 0, :], got[:, 1, :], ALU.add))
            ch.link(V.tensor_tensor(gate_s[:, :], gate_s[:, :], got[:, 2, :], ALU.add))

            def step(j, first=False):
                xs_norm(j + 1)
                h_evac(j)
                if first:
                    dve.wait_ge(s("b2_loaded"), 16)
                add_b2(j - 1)
                result(j - 1)
            for j in range(1, AHEAD - 1):
                dve.wait_ge(rows_got[j + 1], 16)
                step(j, first=j == 1)
            dve.wait_ge(s("later_rows"), 16 * (TOKT - AHEAD))
            with dve.Fori(AHEAD - 1, TOKT - 1) as j:
                step(j)
            h_evac(TOKT - 1)
            add_b2(TOKT - 2)
            add_b2(TOKT - 1)
            result(TOKT - 2)
            result(TOKT - 1)

        @block.tensor
        def _(pe):
            mm = nc.tensor.matmul
            def turn_edges():
                for a in range(2):
                    pe.wait_ge(s("edges_float"), a + 1)
                    for c in range(3):
                        last = nc.tensor.transpose(bankA[a][:, c * P:(c + 1) * P], rawf[:, a, c * P:(c + 1) * P], ident)
                    last.then_inc(s("edges_turned"), 1)

            def turn(c, k):
                pe.wait_ge(s("bank_out"), (c + 1) * QB)
                wait_for(pe, s("turned_out"), c * ROUNDS + k)
                for b in range(k * TURN, min((k + 1) * TURN, SB)):
                    at = (b - k * TURN) * P
                    last = mm(bankR[:, at:at + P], chunk[:, b, :], diff[:, :], start=True, stop=True)
                last.then_inc(s("turned"), 1)

            def tiles(i, g, first, final):
                pe.wait_ge(s("hot_ready"), i * NG + (g + 1))
                pe.wait_ge(s("stairs_ready"), i * NG + (g + 1))
                for r in range(g * GRP, (g + 1) * GRP):
                    for c, q, k0, n, col in segments(r):
                        if (c < 0 and first) or (c > 0 and final):
                            continue
                        start = OPEN[(c, q)] == r and c >= 0 and not (c == 0 and (1, q) in OPEN and not first)
                        if start:
                            if c == 1:
                                pe.wait_ge(s("bank_out"), i * QB + (q + 1))
                            elif not first:
                                pe.wait_ge(s("bank_out"), i * QB + (q + 1 - QB))
                        last = mm(bankA[q][:, col:col + n], ring[:, r, 0:P], ring[:, r, P + k0:P + k0 + n],
                                  start=start, stop=True, skip_group_check=True)
                last.then_inc(s("tiles_done"), 1)

            def body(i, first=False, final=False):
                pe.wait_ge(s("xn_ready"), i + 1)
                for c in range(KC):
                    last = nc.tensor.transpose(bankT[:, c * P:(c + 1) * P], xn[:, c * P:(c + 1) * P], ident)
                last.then_inc(s("xT_turned"), 1)
                if not first:
                    tiles(i, 0, first, final)
                    tiles(i, 1, first, final)
                if first:
                    turn_edges()
                pe.wait_ge(s("xT_ready"), i + 1)
                if not first:
                    pe.wait_ge(s("beta_rest"), i)
                for c in range(KC):
                    if first:
                        pe.wait_ge(wn_loaded[c], 16)
                    last = mm(bankB[:, :], xT[:, c * P:(c + 1) * P], wn_sb[:, c, :], start=c == 0, stop=c == KC - 1)
                last.then_inc(s("beta_done"), 1)
                if not first:
                    turn(i - 1, 0)
                    tiles(i, 2, first, final)
                    tiles(i, 3, first, final)
                    tiles(i, 4, first, final)
                    turn(i - 1, 1)
                    pe.wait_ge(s("alpha_added"), i)
                else:
                    pe.wait_ge(s("wc_loaded"), 16)
                for c in range(KC):
                    last = mm(bankC[:, :], xT[:, c * P:(c + 1) * P], wc_sb[:, c, :], start=c == 0, stop=c == KC - 1)
                last.then_inc(s("alpha_done"), 1)
                if not first:
                    turn(i - 1, 2)
                else:
                    pe.wait_ge(s("src_out"), 1)
                    pe.wait_ge(s("dst_out"), 1)
                    for g in range(4):
                        tiles(i, g, first, final)
                for g in range(4 if first else 5, NG):
                    tiles(i, g, first, final)

            body(0, first=True)
            body(1)
            with pe.Fori(2, NT - 1) as i:
                body(i)
            body(NT - 1, final=True)
            pe.wait_ge(s("alpha_added"), NT)
            pe.wait_ge(s("small_loaded"), 64)
            nc.tensor.transpose(bankC[:, 0:NEXP * KC], b1_rows[:, :], ident[0:NEXP * KC, 0:NEXP * KC]).then_inc(s("b1_turned"), 1)

            def partial(d, par=0):
                for a in range(2):
                    last = mm(bankA[par][:, :], lhs[:, par, d, :], beta[:, a, d, :], start=d == 0 and a == 0,
                              stop=True, skip_group_check=True)
                return last
            pe.wait_ge(s("lhs_ready"), 1)
            pe.wait_ge(s("bank_out"), NT * QB - QB + 1)
            partial(0)
            partial(1)
            turn(NT - 1, 0)
            for d in range(2, 5):
                partial(d)
            turn(NT - 1, 1)
            pe.wait_ge(s("sums_checked"), 1)
            pe.wait_ge(s("beta_rest"), NT)
            mm(bankB[:, 0:2], onesf[:, :], checks[:, :], start=True, stop=True).then_inc(s("checks_summed"), 1)
            partial(5)
            partial(6)
            turn(NT - 1, 2)
            partial(7)
            partial(8)
            pe.wait_ge(s("turned_out"), ROUNDS * NT)

            def second_turn(i):
                pe.wait_ge(s("xn2_ready"), i + 1)
                for c in range(KC):
                    last = nc.tensor.transpose(bankT[:, c * P:(c + 1) * P], xn[:, c * P:(c + 1) * P], ident)
                last.then_inc(s("xn2_turned"), 1)

            def router(i):
                pe.wait_ge(s("xT2_ready"), i + 1)
                for c in range(KC):
                    last = mm(bankB[:, bass.ds(i * NEXP, NEXP)], xT[:, c * P:(c + 1) * P], wr_sb[:, c, :],
                              start=c == 0, stop=c == KC - 1)
                last.then_inc(s("logits_done"), 1)

            pe.wait_ge(s("beta_rest"), NT)
            pe.wait_ge(s("flag_ready"), 1)
            slow = pe.value_load(flag_i[0:1, 0:1], min_val=0, max_val=1 << 30)
            with pe.If(slow == 0):
                def sums(i, par, first=False):
                    for d in range(NT):
                        last = mm(bankA[2 + par][:, 0:1], adj[:, d, bass.ds(i * P, P)], onesb[:, 0:1], start=d == 0,
                                  stop=d == NT - 1, skip_group_check=True)
                    last.then_inc(s("counts_done"), 1)
                    pe.wait_ge(s("lhs_ready"), i + 2)
                    for d in range(NT - 1 if first else 0, NT):
                        last = partial(d, par)
                        if d == HB and not first:
                            second_turn(i - 1)
                    last.then_inc(s("sums_done"), 1)
                    if not first:
                        router(i - 1)
                sums(0, 0, first=True)
                sums(1, 1)
                with pe.Fori(1, NT // 2) as m:
                    for par in range(2):
                        pe.wait_ge(s("x1_ready"), m * 2 + (par - 1))
                        sums(m * 2 + par, par)
                second_turn(NT - 1)
                router(NT - 1)
            with pe.Else():
                acc = [bankA[0], bankA[1], bankA[2], bankA[3], bankT]

                def edge(t, first=False):
                    pe.wait_ge(s("got_rows"), (t + 1) * 16)
                    pe.wait_ge(s("wide_ready"), t + 1)
                    for b in range(HB):
                        hot_b = wide_hot[:, b * P:(b + 1) * P]
                        mm(acc[b][:, :], hot_b, got_row, start=first, stop=True, skip_group_check=True)
                        last = mm(bankB[:, b:b + 1], hot_b, onesf[:, 0:1], start=first and b == 0, stop=True,
                                  skip_group_check=True)
                    last.then_inc(s("edge_summed"), 1)
                for h in range(2):
                    if h:
                        pe.wait_ge(s("slow_x1"), HB)
                    edge(h * ETP, first=True)
                    with pe.Fori(1, ETP) as t:
                        edge(t + h * ETP)
                pe.wait_ge(s("slow_x1"), NT)
                with pe.Fori(0, NT) as i:
                    second_turn(i)
                    router(i)
            pe.nop()

            pe.wait_ge(s("chosen"), 1)
            hv = hot[:, :, :].rearrange("p i e -> p (i e)")
            W = NT * NEXP
            mm(bankC[:, 0:W], trib[:, :], hv, start=True, stop=True, skip_group_check=True)
            for k in range(1, NT):
                mm(bankC[:, k * NEXP:W], onesb[:, :], hv[:, 0:W - k * NEXP], start=False, stop=True,
                   skip_group_check=True)
            for k in range(NT):
                last = mm(bankC[:, P:P + NEXP], onesb[:, :], hv[:, k * NEXP:(k + 1) * NEXP], start=False, stop=True,
                          skip_group_check=True)
            last.then_inc(s("ranked"), 1)

            pe.wait_ge(s("lanes_ready"), 1)

            def to_slots(v, at, n):
                for i in range(NT):
                    last = mm(at, lane_hot[:, i, :], sent[:, i, v:v + n, :].rearrange("p v j -> p (v j)"),
                              start=i == 0 and v > 0, stop=True, skip_group_check=True)
                return last
            pe.wait_ge(s("sent_ready"), 1)
            to_slots(1, bankC[:, 2 * P:2 * P + 2 * TOKT], 2)
            to_slots(0, bankC[:, 2 * P:2 * P + TOKT], 1).then_inc(s("at_slots"), 1)

            def xs_turn(j):
                pe.wait_ge(s("xs_ready"), j + 1)
                for c in range(KC):
                    last = nc.tensor.transpose(bankT[:, c * P:(c + 1) * P], xn[:, c * P:(c + 1) * P], ident)
                last.then_inc(s("xs_turned"), 1)

            def expert_of(j):
                return pe.value_load(exp_i[0:1, bass.ds(j, 1)], min_val=0, max_val=NEXP - 1)

            def up(j):
                e = expert_of(j)
                pe.wait_ge(s("xs_out"), j + 1)
                for c in range(KC):
                    last = mm(bankB[:, :], xT[:, c * P:(c + 1) * P], w1_sb[:, bass.ds(e * (KC * H) + c * H, H)],
                              start=c == 0, stop=c == KC - 1)
                last.then_inc(s("h_done"), 1)

            def down(j):
                e = expert_of(j)
                pe.wait_ge(s("hT_ready"), j + 1)
                wait_for(pe, s("y_ready"), j)
                for c in range(KC):
                    last = mm(bankA[0][:, :], hidT[:, c * P:(c + 1) * P], w2_sb[:, bass.ds(e * (KC * H) + c * H, H)],
                              start=c == 0, stop=c == KC - 1)
                last.then_inc(s("y_done"), 1)

            def h_turn(j):
                pe.wait_ge(s("h_out"), j + 1)
                for c in range(KC):
                    last = nc.tensor.transpose(bankC[:, c * P:(c + 1) * P], hid[:, c * P:(c + 1) * P], ident)
                last.then_inc(s("h_turned"), 1)

            pe.wait_ge(s("experts_ready"), 1)
            xs_turn(0)
            pe.wait_ge(s("w1_loaded"), 16 * NEXP)
            up(0)
            xs_turn(1)
            pe.wait_ge(s("sent_ready"), 2)
            to_slots(3, bankR[:, 0:3 * TOKT], 3).then_inc(s("at_slots"), 1)
            h_turn(0)
            up(1)
            xs_turn(2)
            pe.wait_ge(s("w2_loaded"), 16 * NEXP)
            down(0)
            h_turn(1)
            with pe.Fori(2, TOKT - 1) as j:
                up(j)
                xs_turn(j + 1)
                down(j - 1)
                h_turn(j)
            up(TOKT - 1)
            down(TOKT - 2)
            h_turn(TOKT - 1)
            down(TOKT - 1)


_INS = ['x', 'src', 'dst', 'L0_gnn_wc', 'L0_gnn_wn', 'L0_gnn_bias', 'L0_ffn_Wr', 'L0_ffn_br', 'L0_ffn_W1', 'L0_ffn_b1',
        'L0_ffn_W2', 'L0_ffn_b2']


def kernel(**inputs):
    import concourse.bacc as _bacc
    from concourse.bass_utils import run_bass_kernel_spmd as _run

    nc = _bacc.Bacc("TRN2", target_bir_lowering=False, num_devices=1, dynamic_dma_scratch_size=8192)
    arrays, args = {}, []
    for name in _INS:
        a = np.ascontiguousarray(inputs[name])
        arrays[f"in_{name}"] = a
        args.append(nc.dram_tensor(f"in_{name}", a.shape, mybir.dt.from_np(a.dtype), kind="ExternalInput").ap())
    t = tables()
    arrays["tables"] = t
    args.append(nc.dram_tensor("tables", t.shape, mybir.dt.float32, kind="ExternalInput").ap())
    args.append(nc.dram_tensor("result", (N, H), mybir.dt.float32, kind="ExternalOutput").ap())
    build(nc, *args)
    r = _run(nc, [arrays], core_ids=[0])
    return r.results[0]["result"]
```
